# Optimizing a Trainium2 kernel written in Bass

```python
import numpy as np
import jax
import jax.numpy as jnp

def _softmax(x, axis=-1):
    return jax.nn.softmax(x, axis=axis)

def _gelu(x):
    return jax.nn.gelu(x, approximate=True)

def _silu(x):
    return jax.nn.silu(x)

def _sigmoid(x):
    return jax.nn.sigmoid(x)

def _layernorm(x, axis=-1, eps=1e-05):
    m = jnp.mean(x, axis=axis, keepdims=True)
    v = jnp.var(x, axis=axis, keepdims=True)
    return (x - m) / jnp.sqrt(v + eps)

def _scatter_add(tgt, idx, src, axis=0):
    return tgt.at[idx].add(src)

def _segment_sum(src, seg, n):
    return jax.ops.segment_sum(src, seg, n)
kernel_name = 'mk_adaln_d1_jaxref_r8_1c8102'

def setup_inputs(seed: int=0):
    np.random.seed(seed)
    _w = jnp.asarray

    def _L0_attn_setup():
        import jax, jax.numpy as jnp
        import numpy as np
        DIM = 256
        SEGMENT_LEN = 128
        HEADS = 32
        DIM_HEAD = 64
        P = 16
        SCALE = 1.0 / np.sqrt(DIM_HEAD)
        key = jax.random.key(seed)
        ks = jax.random.split(key, 4)
        seq = jax.random.normal(ks[0], (2, 1024, DIM), dtype=jnp.float32)
        w_norm = jnp.ones((DIM,), dtype=jnp.float32)
        w_qkv = jax.random.normal(ks[1], (DIM, 3 * HEADS * DIM_HEAD), dtype=jnp.float32) * 0.02
        w_out = jax.random.normal(ks[2], (HEADS * DIM_HEAD, DIM), dtype=jnp.float32) * 0.02
        pm = jax.random.normal(ks[3], (2, HEADS, P, DIM_HEAD), dtype=jnp.float32) * 0.02
        return {'seq': seq, 'w_norm': w_norm, 'w_qkv': w_qkv, 'w_out': w_out, 'pm': pm}
    _L0_attn_in = _L0_attn_setup()

    def _L0_ffn_setup():
        import jax, jax.numpy as jnp
        import numpy as np

        def _sparsify_2to4(h):
            B, S, I = h.shape
            g = h.reshape(B, S, I // 4, 4)
            a = jnp.abs(g)
            _, idx = jax.lax.top_k(a, 2)
            pos = jnp.arange(4)
            mask = (pos == idx[..., 0:1]) | (pos == idx[..., 1:2])
            return (g * mask.astype(g.dtype)).reshape(B, S, I)
        key = jax.random.key(seed)
        k1, k2, k3, k4 = jax.random.split(key, 4)
        B, S, H, I = (4, 256, 256, 1024)
        x = jax.random.normal(k1, (B, S, H), dtype=jnp.float32)
        w_gate = jax.random.normal(k2, (H, I), dtype=jnp.float32) / np.sqrt(H)
        w_up = jax.random.normal(k3, (H, I), dtype=jnp.float32) / np.sqrt(H)
        w_down = jax.random.normal(k4, (I, H), dtype=jnp.float32) / np.sqrt(I)
        return {'x': x, 'w_gate': w_gate, 'w_up': w_up, 'w_down': w_down}
    _L0_ffn_in = _L0_ffn_setup()
    _L0_c = _w((lambda *s: np.random.randn(*s).astype(np.float32) * 0.05)(2, 256))
    _L0_wmod = _w((lambda *s: np.random.randn(*s).astype(np.float32) * 0.05)(256, 6 * 256) * 256 ** (-0.5))
    _d = {'L0_attn_seq': _L0_attn_in['seq'], 'L0_attn_w_norm': _L0_attn_in['w_norm'], 'L0_attn_w_qkv': _L0_attn_in['w_qkv'], 'L0_attn_w_out': _L0_attn_in['w_out'], 'L0_attn_pm': _L0_attn_in['pm'], 'L0_ffn_w_gate': _L0_ffn_in['w_gate'], 'L0_ffn_w_up': _L0_ffn_in['w_up'], 'L0_ffn_w_down': _L0_ffn_in['w_down'], 'L0_c': _L0_c, 'L0_wmod': _L0_wmod}
    _x0 = _d['L0_attn_seq']
    _d['L0_attn_seq'] = jax.random.normal(jax.random.fold_in(jax.random.key(seed), 1), (2, 1024, 256), dtype=_x0.dtype)
    del _x0
    return _d

def reference(L0_attn_seq, L0_attn_w_norm, L0_attn_w_qkv, L0_attn_w_out, L0_attn_pm, L0_ffn_w_gate, L0_ffn_w_up, L0_ffn_w_down, L0_c, L0_wmod):

    def _L0_attn_ref(seq, w_norm, w_qkv, w_out, pm):
        import jax, jax.numpy as jnp
        import numpy as np
        DIM = 256
        SEGMENT_LEN = 128
        HEADS = 32
        DIM_HEAD = 64
        P = 16
        SCALE = 1.0 / np.sqrt(DIM_HEAD)
        b, seq_len, d = seq.shape
        next_len = -(-seq_len // SEGMENT_LEN) * SEGMENT_LEN
        pad = next_len - seq_len
        x = jnp.pad(seq, ((0, 0), (0, pad), (0, 0))) if pad > 0 else seq
        w = next_len // SEGMENT_LEN
        x = x.reshape(b * SEGMENT_LEN, w, d)
        eps = jnp.finfo(x.dtype).eps
        x = x * jax.lax.rsqrt(jnp.mean(jnp.square(x), axis=-1, keepdims=True) + eps) * w_norm
        qkv = x @ w_qkv
        q, k, v = jnp.split(qkv, 3, axis=-1)
        B = x.shape[0]
        split = lambda t: t.reshape(B, w, HEADS, DIM_HEAD).transpose(0, 2, 1, 3)
        q, k, v = (split(q), split(k), split(v))
        pmk = jnp.broadcast_to(pm[0], (B, HEADS, P, DIM_HEAD))
        pmv = jnp.broadcast_to(pm[1], (B, HEADS, P, DIM_HEAD))
        k = jnp.concatenate([pmk, k], axis=2)
        v = jnp.concatenate([pmv, v], axis=2)
        scores = jnp.einsum('bhqd,bhkd->bhqk', q, k) * SCALE
        mask = jnp.arange(P + w)[None, :] <= jnp.arange(w)[:, None]
        scores = jnp.where(mask, scores, jnp.finfo(scores.dtype).min)
        attn = jax.nn.softmax(scores, axis=-1)
        out = jnp.einsum('bhqk,bhkd->bhqd', attn, v)
        out = out.transpose(0, 2, 1, 3).reshape(B, w, HEADS * DIM_HEAD)
        out = out @ w_out
        out = out.reshape(b, SEGMENT_LEN * w, d)
        return out[:, :seq_len]

    def _L0_ffn_ref(x, w_gate, w_up, w_down):
        import jax, jax.numpy as jnp
        import numpy as np

        def _sparsify_2to4(h):
            B, S, I = h.shape
            g = h.reshape(B, S, I // 4, 4)
            a = jnp.abs(g)
            _, idx = jax.lax.top_k(a, 2)
            pos = jnp.arange(4)
            mask = (pos == idx[..., 0:1]) | (pos == idx[..., 1:2])
            return (g * mask.astype(g.dtype)).reshape(B, S, I)
        h = jax.nn.silu(jnp.einsum('bsh,hi->bsi', x, w_gate)) * jnp.einsum('bsh,hi->bsi', x, w_up)
        h_sparse = _sparsify_2to4(h)
        return jnp.einsum('bsi,ih->bsh', h_sparse, w_down)
    x = L0_attn_seq
    mod = (_silu(L0_c) @ L0_wmod).reshape(L0_c.shape[0], 6, 1, -1)
    sa, ca, ga, sb, cb, gb = (mod[:, 0], mod[:, 1], mod[:, 2], mod[:, 3], mod[:, 4], mod[:, 5])
    ga = (2 * (ga >= 0) - 1) * jnp.maximum(jnp.abs(ga), 0.25)
    gb = (2 * (gb >= 0) - 1) * jnp.maximum(jnp.abs(gb), 0.25)
    h = _layernorm(x, axis=-1) * (1 + ca) + sa
    x = x + ga * _L0_attn_ref(h, L0_attn_w_norm, L0_attn_w_qkv, L0_attn_w_out, L0_attn_pm)
    h = _layernorm(x, axis=-1) * (1 + cb) + sb
    x = x + gb * _L0_ffn_ref(h, L0_ffn_w_gate, L0_ffn_w_up, L0_ffn_w_down)
    return x

_drawn_inputs = setup_inputs


def setup_inputs(seed=0):
    import zlib

    import numpy as np

    out = dict(_drawn_inputs(seed))
    spreads = {'L0_attn_w_norm': (1.0, 0.6)}
    factors = {'L0_attn_w_qkv': 8.0, 'L0_attn_w_out': 8.0, 'L0_attn_pm': 8.0}
    for name, (base, spread) in spreads.items():
        noise = np.random.default_rng([zlib.crc32(name.encode()), seed]).standard_normal(out[name].shape)
        drawn = base * np.exp(spread * noise) if base else spread * noise
        out[name] = jnp.asarray(drawn.astype(out[name].dtype))
    for name, factor in factors.items():
        out[name] = (out[name] * factor).astype(out[name].dtype)
    return out
```

```python
from contextlib import ExitStack

import concourse.bass as bass
from concourse import mybir

ALU = mybir.AluOpType
ACT = mybir.ActivationFunctionType
F32 = mybir.dt.float32
BF16 = mybir.dt.bfloat16
I32 = mybir.dt.int32
AX_X = mybir.AxisListType.X

P = 128
HEADS = 32
DH = 64
MEM = 16
SEGMENT = 128
EPS_LN = 1e-5
EPS_RMS = 2.0 ** -23
SHIFT_A, SCALE_A, GATE_A, SHIFT_B, SCALE_B, GATE_B = range(6)
RSQRT_SEED = 0x5F3759DF


def adaln_block(nc, seq, w_norm, wqT, w_out, pmkT, pmvT, w_gate, w_up, w_down, cT, w_mod, out):
    B, S, D = seq.shape
    W = S // SEGMENT
    KD = D // P
    HP = HEADS // 2
    NK = W * HEADS
    SETS = 2
    T = 4 * P
    NB = B * S // T
    SCALE = float(DH) ** -0.5
    assert (D, KD, W, NB, B) == (256, 2, 8, 4, 2) and S == P * W

    with ExitStack() as ctx:
        def sb(name, shape, dt=F32):
            return ctx.enter_context(nc.sbuf_tensor(name, shape, dt))

        def sem(name):
            return ctx.enter_context(nc.semaphore(name))

        x = sb("x", [P, NB, 4, D])
        z = sb("z", [P, NB, 4, D])
        hT = sb("hT", [P, KD, NB, T])
        h2T = sb("h2T", [P, KD, NB, T])
        wq_sb = sb("wq_sb", [P, HP, D])
        wo_sb = sb("wo_sb", [P, HP, D])
        wmod_sb = sb("wmod_sb", [P, KD, 6 * D])
        wg_sb = sb("wg_sb", [P, KD, SETS, 4, P])
        wu_sb = sb("wu_sb", [P, KD, SETS, 4, P])
        wd_sb = sb("wd_sb", [P, SETS, 4, D])
        pm_sb = sb("pm_sb", [P, 2, HP, W])
        pair = sb("pair", [P, 2, HP, 2, W])
        W1 = sb("W1", [P, KD, NK])
        W2T = sb("W2T", [P, B, KD, NK])
        W2 = sb("W2", [P, B, 2, D])
        wn = sb("wn", [P, KD])
        c_sb = sb("c_sb", [P, KD, B])
        c_e = sb("c_e", [P, KD, B])
        c_silu = sb("c_silu", [P, KD, B])
        mod = sb("mod", [P, 6, KD, B])
        gate_abs = sb("gate_abs", [P, KD, B])
        gate_sign = sb("gate_sign", [P, KD, B])
        gateB = sb("gateB", [P, KD, NB])
        ident = sb("ident", [P, P])
        ones = sb("ones", [P, 1])
        stats = sb("stats", [P, 16, 6])
        mv = sb("mv", [P, 16, 2])
        var = sb("var", [P, 16])
        rstd = sb("rstd", [P, 16])
        newton = sb("newton", [P, 2, 16])
        seed = sb("seed", [P, 16], I32)
        rms = sb("rms", [P, 16])
        sq = sb("sq", [P, 2, KD, T])
        top = sb("top", [P, 2, B, HEADS])
        diff = sb("diff", [P, 2, B, NK])
        ex = sb("ex", [P, 2, B, NK])
        total = sb("total", [P, 2, B, HEADS])
        inv = sb("inv", [P, 2, B, HEADS])
        prob = sb("prob", [P, 2, B, NK])
        probT = sb("probT", [P, 2, 2, B, P])
        sg = sb("sg", [P, 2, T])
        beats = sb("beats", [P, 6, T], BF16)
        pairs = sb("pairs", [P, 4, T], BF16)
        wins = sb("wins", [P, 4, T], BF16)
        yT = sb("yT", [P, KD, T])

        hid = wq_sb[:, :, :].rearrange("p a b -> p (a b)").rearrange("p (s r t) -> p s r t", s=2, r=4)
        mag = wo_sb[:, :, :].rearrange("p a b -> p (a b)").rearrange("p (s r t) -> p s r t", s=2, r=4)
        kept = hT[:, :, :, :]

        ps = ctx.enter_context(nc.psum_tensor("ps", [P, 8, T], F32))
        modP = ps[:, 0, 0:6 * KD * B].rearrange("p (m k b) -> p m k b", m=6, k=KD)
        sumP = ps[:, 1, 0:16]

        ld_c = sem("ld_c"); ld_mod = sem("ld_mod"); ld_x = [sem(f"ld_x{q}") for q in range(NB)]
        ld_pm = sem("ld_pm"); ld_wq = sem("ld_wq"); ld_wo = sem("ld_wo"); ld_wn = sem("ld_wn")
        ld_wg = sem("ld_wg"); ld_wu = sem("ld_wu"); ld_wd = sem("ld_wd")
        zeroed = sem("zeroed"); ident_ok = sem("ident_ok"); ones_ok = sem("ones_ok"); pair_ok = sem("pair_ok")
        c_exp = sem("c_exp"); c_ok = sem("c_ok")
        mod_mm = sem("mod_mm"); mod_ok = sem("mod_ok")
        z_ok = sem("z_ok"); zT_mm = sem("zT_mm"); hT_ok = sem("hT_ok"); sq_ok = sem("sq_ok")
        sum_mm = sem("sum_mm"); rms_ok = sem("rms_ok")
        W1_mm = sem("W1_mm"); W1_ok = sem("W1_ok"); W2T_mm = sem("W2T_mm"); W2T_ok = sem("W2T_ok")
        W2_mm = sem("W2_mm"); W2_ok = sem("W2_ok")
        score_mm = sem("score_mm"); diff_ok = sem("diff_ok"); exp_ok = sem("exp_ok"); prob_ok = sem("prob_ok")
        probT_mm = sem("probT_mm"); probT_ok = sem("probT_ok"); att_mm = sem("att_mm"); x1_ok = sem("x1_ok")
        z2_ok = sem("z2_ok"); z2T_mm = sem("z2T_mm"); h2T_ok = sem("h2T_ok")
        gate_mm = sem("gate_mm"); up_mm = sem("up_mm"); silu_ok = sem("silu_ok"); hid_ok = sem("hid_ok")
        mag_ok = sem("mag_ok"); beats_ok = sem("beats_ok"); pairs_ok = sem("pairs_ok"); wins_ok = sem("wins_ok")
        kept_ok = sem("kept_ok"); down_mm = sem("down_mm"); yT_ok = sem("yT_ok"); back_mm = sem("back_mm")
        y_ok = sem("y_ok"); stored = sem("stored"); dve_step = sem("dve_step")

        block = ctx.enter_context(nc.Block())

        def widths(i):
            n = HEADS * (i + 1)
            return [min(P, n)] + ([n - P] if n > P else [])

        @block.sync
        def _(sp):
            sp.dma_start(c_sb[:, :, :], cT.rearrange("(k p) b -> p k b", p=P)).then_inc(ld_c, 16)
            sp.dma_start(wmod_sb[:, :, :], w_mod.rearrange("(k p) n -> p k n", p=P)).then_inc(ld_mod, 16)
            rows = seq.rearrange("b (p f i) d -> f b p i d", f=2, i=4)
            for q in range(NB):
                sp.dma_start(x[:, q, :, :], rows[q // B, q % B]).then_inc(ld_x[q], 16)
            sp.dma_start(pm_sb[:, 0, :, :], pmkT).then_inc(ld_pm, 16)
            sp.dma_start(pm_sb[:, 1, :, :], pmvT).then_inc(ld_pm, 16)
            sp.dma_start(wq_sb[:, :, :], wqT.rearrange("(g p) d -> p g d", p=P)).then_inc(ld_wq, 16)
            sp.dma_start(wn[:, :], w_norm.rearrange("(k p) -> p k", p=P),
                         allow_slow_non_contiguous=True).then_inc(ld_wn, 16)
            sp.dma_start(wo_sb[:, :, :], w_out.rearrange("(g p) d -> p g d", p=P)).then_inc(ld_wo, 16)
            sp.dma_start(wg_sb[:, :, :, :, :], w_gate.rearrange("(k p) s r g -> p k s r g", p=P)).then_inc(ld_wg, 16)
            sp.dma_start(wu_sb[:, :, :, :, :], w_up.rearrange("(k p) s r g -> p k s r g", p=P)).then_inc(ld_wu, 16)
            sp.dma_start(wd_sb[:, :, :, :], w_down.rearrange("(s g r) d -> g s r d", s=SETS, r=4)).then_inc(ld_wd, 16)
            dest = out.rearrange("b (p f i) d -> f b p i d", f=2, i=4)
            for q in range(NB):
                sp.wait_ge(y_ok, 2 * (q + 1))
                sp.dma_start(dest[q // B, q % B], x[:, q, :, :]).then_inc(stored, 16)
            sp.wait_ge(stored, 16 * NB)

        @block.gpsimd
        def _(pool):
            nc.gpsimd.memset(ident[:, :], 0.0).then_inc(zeroed, 1)
            nc.gpsimd.memset(pair[:, :, :, :, :], 0.0).then_inc(zeroed, 1)
            nc.gpsimd.memset(ones[:, :], 1.0).then_inc(ones_ok, 1)
            pool.wait_ge(zeroed, 1)
            nc.gpsimd.affine_select(out=ident[:, :], in_=ident[:, :], compare_op=ALU.not_equal, fill=1.0,
                                    base=0, pattern=[[-1, P]], channel_multiplier=1).then_inc(ident_ok, 1)
            pool.wait_ge(zeroed, 2)
            pool.wait_ge(ld_pm, 32)
            pool.wait_ge(ident_ok, 1)
            for r in range(2):
                if r:
                    pool.wait_ge(pair_ok, r)
                nc.gpsimd.tensor_copy(pair[DH * r:DH * (r + 1), :, :, r, :],
                                      pm_sb[DH * r:DH * (r + 1), :, :, :]).then_inc(pair_ok, 1)

        @block.scalar
        def _(act):
            act.wait_ge(ld_c, 16)
            nc.scalar.activation(c_e[:, :, :], c_sb[:, :, :], ACT.Exp, scale=-1.0).then_inc(c_exp, 1)
            act.wait_ge(mod_ok, 1)
            for q in range(NB):
                for k in range(KD):
                    act.wait_ge(zT_mm, KD * q + k + 1)
                    nc.scalar.activation(hT[:, k, q, :], ps[:, 6 + k, :], ACT.Identity,
                                         scale=mod[:, SCALE_A, k, q % B:q % B + 1],
                                         bias=mod[:, SHIFT_A, k, q % B:q % B + 1]).then_inc(hT_ok, 1)
                if q >= 2:
                    act.wait_ge(sum_mm, q - 1)
                act.wait_ge(hT_ok, KD * (q + 1))
                nc.scalar.activation(sq[:, q % 2, :, :], hT[:, :, q, :], ACT.Square).then_inc(sq_ok, 1)
            for b in range(B):
                act.wait_ge(W2_mm, b + 1)
                nc.scalar.activation(W2[:, b, :, :], ps[:, 2 + b, :].rearrange("p (c d) -> p c d", c=2),
                                     ACT.Copy).then_inc(W2_ok, 1)
            act.wait_ge(rms_ok, 1)

            def exps(i):
                n = HEADS * (i + 1)
                act.wait_ge(diff_ok, i + 1)
                if i >= 2:
                    act.wait_ge(prob_ok, i - 1)
                for b in range(B):
                    tile = 4 * (B * (i // 4) + b) + i % 4
                    nc.scalar.activation(ex[:, i % 2, b, 0:n], diff[:, i % 2, b, 0:n], ACT.Exp,
                                         scale=rms[:, tile:tile + 1]).then_inc(exp_ok, 1)

            def take_probT(i):
                act.wait_ge(probT_mm, i + 1)
                if i >= 2:
                    act.wait_ge(att_mm, i - 1)
                for c, w in enumerate(widths(i)):
                    last = nc.scalar.activation(probT[0:w, i % 2, c, :, :],
                                                ps[0:w, 2 + i % 2, 2 * P * c:2 * P * (c + 1)]
                                                .rearrange("p (b t) -> p b t", b=B), ACT.Copy)
                last.then_inc(probT_ok, 1)

            def take_h2T(f):
                for q in (B * f, B * f + 1):
                    for k in range(KD):
                        act.wait_ge(z2T_mm, KD * q + k + 1)
                        nc.scalar.activation(h2T[:, k, q, :], ps[:, 6 + k, :], ACT.Identity,
                                             scale=mod[:, SCALE_B, k, q % B:q % B + 1],
                                             bias=mod[:, SHIFT_B, k, q % B:q % B + 1]).then_inc(h2T_ok, 1)

            for t in range(W + 2):
                if t < W:
                    exps(t)
                if 1 <= t <= W:
                    take_probT(t - 1)
                if t == 6:
                    take_h2T(0)
            take_h2T(1)

            def silus(q, s, first):
                u = q * (SETS * 4) + 4 * s
                for r in range(5):
                    if r < 4:
                        act.wait_ge(gate_mm, u + r + 1)
                        if not (first and s == 0 and r < 2):
                            act.wait_ge(hid_ok, u + r - 1)
                        nc.scalar.activation(sg[:, r % 2, :], ps[:, r % 2, :], ACT.Silu).then_inc(silu_ok, 1)
                    if r == 1 and not first:
                        act.wait_ge(beats_ok, (q * SETS + s - 1) * 3)
                    if r >= 1:
                        act.wait_ge(hid_ok, u + r)
                        nc.scalar.activation(mag[:, s, r - 1, :], hid[:, s, r - 1, :], ACT.Abs).then_inc(mag_ok, 1)

            def take_y(q):
                act.wait_ge(down_mm, SETS * q + SETS)
                for k in range(KD):
                    nc.scalar.activation(yT[:, k, :], ps[:, 4 + k, :], ACT.Identity,
                                         scale=gateB[:, k, bass.ds(q, 1)]).then_inc(yT_ok, 1)

            silus(0, 0, True)
            silus(0, 1, True)
            with act.Fori(1, NB) as q:
                silus(q, 0, False)
                act.wait_ge(down_mm, SETS * q)
                for k in range(KD):
                    nc.scalar.activation(yT[:, k, :], ps[:, 4 + k, :], ACT.Identity,
                                         scale=gateB[:, k, bass.ds(q - 1, 1)]).then_inc(yT_ok, 1)
                silus(q, 1, False)
            take_y(NB - 1)

        @block.tensor
        def _(pe):
            pe.wait_ge(c_ok, 1)
            pe.wait_ge(ld_mod, 16)
            for m in range(6):
                for n in range(KD):
                    for k in range(KD):
                        last = nc.tensor.matmul(modP[:, m, n, :], wmod_sb[:, k, (m * KD + n) * P:(m * KD + n + 1) * P],
                                                c_silu[:, k, :], start=(k == 0), stop=(k == KD - 1))
            last.then_inc(mod_mm, 1)
            pe.wait_ge(ident_ok, 1)
            for q in range(NB):
                pe.wait_ge(z_ok, q + 1)
                for k in range(KD):
                    if q >= 1:
                        pe.wait_ge(hT_ok, KD * (q - 1) + k + 1)
                    for t in range(4):
                        last = nc.tensor.transpose(ps[:, 6 + k, P * t:P * (t + 1)],
                                                   z[:, q, t, P * k:P * (k + 1)], ident[:, :])
                    last.then_inc(zT_mm, 1)
            pe.wait_ge(pair_ok, 2)
            pe.wait_ge(ld_wq, 16)
            for k in range(KD):
                for g in range(HP):
                    last = nc.tensor.matmul(ps[:, 4, NK * k + 2 * W * g:NK * k + 2 * W * (g + 1)],
                                            wq_sb[:, g, P * k:P * (k + 1)], pair[:, 0, g, :, :],
                                            start=True, stop=True)
            last.then_inc(W1_mm, 1)
            pe.wait_ge(ones_ok, 1)
            for q in range(NB):
                pe.wait_ge(sq_ok, q + 1)
                for t in range(4):
                    for k in range(KD):
                        last = nc.tensor.matmul(sumP[:, 4 * q + t:4 * q + t + 1], sq[:, q % 2, k, P * t:P * (t + 1)],
                                                ones[:, :], start=(k == 0), stop=(k == KD - 1))
                last.then_inc(sum_mm, 1)
            pe.wait_ge(ld_wo, 16)
            for k in range(KD):
                for g in range(HP):
                    last = nc.tensor.matmul(ps[:, 5, NK * k + 2 * W * g:NK * k + 2 * W * (g + 1)],
                                            wo_sb[:, g, P * k:P * (k + 1)], pair[:, 1, g, :, :],
                                            start=True, stop=True)
            last.then_inc(W2T_mm, 1)
            for b in range(B):
                pe.wait_ge(W2T_ok, KD * (b + 1))
                for c in range(2):
                    for k in range(KD):
                        last = nc.tensor.transpose(ps[:, 2 + b, D * c + P * k:D * c + P * (k + 1)],
                                                   W2T[:, b, k, P * c:P * (c + 1)], ident[:, :])
                last.then_inc(W2_mm, 1)

            def scores(i):
                n = HEADS * (i + 1)
                if i >= 2:
                    pe.wait_ge(diff_ok, i - 1)
                for b in range(B):
                    q = B * (i // 4) + b
                    for k in range(KD):
                        last = nc.tensor.matmul(ps[:, i % 2, D * b:D * b + n], hT[:, k, q, P * (i % 4):P * (i % 4 + 1)],
                                                W1[:, k, 0:n], start=(k == 0), stop=(k == KD - 1))
                last.then_inc(score_mm, 1)

            def turn_probs(i):
                pe.wait_ge(prob_ok, i + 1)
                if i >= 2:
                    pe.wait_ge(probT_ok, i - 1)
                for c, w in enumerate(widths(i)):
                    for b in range(B):
                        last = nc.tensor.transpose(ps[0:w, 2 + i % 2, P * (2 * c + b):P * (2 * c + b + 1)],
                                                   prob[:, i % 2, b, P * c:P * c + w], ident[:, :])
                last.then_inc(probT_mm, 1)

            def attend(i):
                pe.wait_ge(probT_ok, i + 1)
                if i >= 2:
                    pe.wait_ge(x1_ok, i - 1)
                ws = widths(i)
                for b in range(B):
                    for c, w in enumerate(ws):
                        last = nc.tensor.matmul(ps[:, 4 + i % 2, D * b:D * (b + 1)], probT[0:w, i % 2, c, b, :],
                                                W2[0:w, b, c, :], start=(c == 0), stop=(c == len(ws) - 1))
                last.then_inc(att_mm, 1)

            def turn_z2(f):
                for q in (B * f, B * f + 1):
                    pe.wait_ge(z2_ok, q + 1)
                    for k in range(KD):
                        if q == 0:
                            pe.wait_ge(hT_ok, KD * (NB - 1) + k + 1)
                        else:
                            pe.wait_ge(h2T_ok, KD * (q - 1) + k + 1)
                        for t in range(4):
                            last = nc.tensor.transpose(ps[:, 6 + k, P * t:P * (t + 1)],
                                                       z[:, q, t, P * k:P * (k + 1)], ident[:, :])
                        last.then_inc(z2T_mm, 1)

            pe.wait_ge(W1_ok, KD)
            pe.wait_ge(rms_ok, 1)
            pe.wait_ge(W2_ok, B)
            scores(0)
            scores(1)
            for i in range(W):
                turn_probs(i)
                if i + 2 < W:
                    scores(i + 2)
                attend(i)
                if i == 5:
                    turn_z2(0)
            turn_z2(1)

            pe.wait_ge(ld_wg, 16)
            pe.wait_ge(ld_wu, 16)
            pe.wait_ge(ld_wd, 16)
            pe.wait_ge(diff_ok, W)
            pe.wait_ge(probT_ok, W)
            pe.wait_ge(x1_ok, W)
            pe.wait_ge(h2T_ok, KD * NB)

            def gate_up(q, s, first):
                u = q * (SETS * 4) + 4 * s
                early = first and s == 0
                for r in range(4):
                    if not (early and r < 2):
                        pe.wait_ge(silu_ok, u + r - 1)
                    for k in range(KD):
                        last = nc.tensor.matmul(ps[:, r % 2, :], wg_sb[:, k, s, r, :], h2T[:, k, q, :],
                                                start=(k == 0), stop=(k == KD - 1))
                    last.then_inc(gate_mm, 1)
                    if not (early and r < 2):
                        pe.wait_ge(hid_ok, u + r - 1)
                    for k in range(KD):
                        last = nc.tensor.matmul(ps[:, 2 + r % 2, :], wu_sb[:, k, s, r, :], h2T[:, k, q, :],
                                                start=(k == 0), stop=(k == KD - 1))
                    last.then_inc(up_mm, 1)

            def down(unit, s, yT_before):
                if s == 0 and yT_before is not None:
                    pe.wait_ge(yT_ok, yT_before)
                for r in range(4):
                    pe.wait_ge(kept_ok, unit * 4 + r + 1)
                    for k in range(KD):
                        last = nc.tensor.matmul(ps[:, 4 + k, :], wd_sb[:, s, r, P * k:P * (k + 1)], kept[:, s, r, :],
                                                start=(s == 0 and r == 0), stop=(s == SETS - 1 and r == 3))
                last.then_inc(down_mm, 1)

            def turn_y(yT_count):
                pe.wait_ge(yT_ok, yT_count)
                for t in range(4):
                    for k in range(KD):
                        last = nc.tensor.transpose(ps[:, 6 + t // 2, D * (t % 2) + P * k:D * (t % 2) + P * (k + 1)],
                                                   yT[:, k, P * t:P * (t + 1)], ident[:, :])
                    if t % 2:
                        last.then_inc(back_mm, 1)

            gate_up(0, 0, True)
            gate_up(0, 1, True)
            down(0, 0, None)
            with pe.Fori(1, NB) as q:
                gate_up(q, 0, False)
                down(q * SETS - 1, 1, None)
                gate_up(q, 1, False)
                turn_y(q * KD)
                down(q * SETS, 0, q * KD)
            down(NB * SETS - 1, 1, None)
            pe.wait_ge(y_ok, 2 * (NB - 1))
            turn_y(NB * KD)

        @block.vector
        def _(dve):
            steps = [0]

            def link(ins):
                steps[0] += 1
                ins.then_inc(dve_step, 1)
                dve.wait_ge(dve_step, steps[0])

            def rsqrt(dst, src, n):
                bits, half, yy = seed[:, 0:n], newton[:, 0, 0:n], newton[:, 1, 0:n]
                link(nc.vector.tensor_scalar(bits, src.bitcast(I32), 1, None, ALU.arith_shift_right))
                link(nc.vector.tensor_scalar(dst.bitcast(I32), bits, -1.0, float(RSQRT_SEED), ALU.mult, ALU.add))
                link(nc.vector.tensor_scalar(half, src, -0.5, None, ALU.mult))
                for _ in range(4):
                    link(nc.vector.tensor_tensor(yy, dst, dst, ALU.mult))
                    link(nc.vector.tensor_tensor(yy, yy, half, ALU.mult))
                    link(nc.vector.scalar_tensor_tensor(dst, yy, 1.5, dst, ALU.add, ALU.mult))

            def tile_stats(q, t):
                return nc.vector.bn_stats(stats[:, 4 * q + t, :], x[:, q, t, :])

            def normalise(q0, nq):
                a, b = 4 * q0, 4 * (q0 + nq)
                for t in range(a, b):
                    last = nc.vector.bn_aggr(mv[:, t, :], stats[:, t, :])
                link(last)
                link(nc.vector.tensor_scalar(var[:, a:b], mv[:, a:b, 1], EPS_LN, None, ALU.add))
                rsqrt(rstd[:, a:b], var[:, a:b], b - a)
                for t in range(a, b):
                    yield t, nc.vector.tensor_scalar(z[:, t // 4, t % 4, :], x[:, t // 4, t % 4, :],
                                                     mv[:, t, 0:1], rstd[:, t:t + 1], ALU.subtract, ALU.mult)

            dve.wait_ge(c_exp, 1)
            link(nc.vector.tensor_scalar(c_e[:, :, :], c_e[:, :, :], 1.0, None, ALU.add))
            link(nc.vector.reciprocal(c_e[:, :, :], c_e[:, :, :]))
            nc.vector.tensor_tensor(c_silu[:, :, :], c_sb[:, :, :], c_e[:, :, :], ALU.mult).then_inc(c_ok, 1)

            def first_norm(q0, nq):
                for q in range(q0, q0 + nq):
                    dve.wait_ge(ld_x[q], 16)
                    for t in range(4):
                        last = tile_stats(q, t)
                link(last)
                for t, ins in normalise(q0, nq):
                    if t % 4 == 3:
                        ins.then_inc(z_ok, 1)

            first_norm(0, 2)
            dve.wait_ge(mod_mm, 1)
            link(nc.vector.tensor_copy(mod[:, :, :, :], modP))
            for m in (SCALE_A, SCALE_B):
                link(nc.vector.tensor_scalar(mod[:, m, :, :], mod[:, m, :, :], 1.0, None, ALU.add))
            for m in (GATE_A, GATE_B):
                g = mod[:, m, :, :]
                link(nc.vector.scalar_tensor_tensor(gate_abs[:, :, :], g, -1.0, g, ALU.mult, ALU.max))
                link(nc.vector.tensor_scalar(gate_abs[:, :, :], gate_abs[:, :, :], 0.25, None, ALU.max))
                link(nc.vector.tensor_scalar(gate_sign[:, :, :], g, 0.0, 2.0, ALU.is_ge, ALU.mult))
                link(nc.vector.scalar_tensor_tensor(g, gate_sign[:, :, :], 1.0, gate_abs[:, :, :],
                                                    ALU.subtract, ALU.mult))
            for f in range(NB // B):
                last = nc.vector.tensor_copy(gateB[:, :, B * f:B * (f + 1)], mod[:, GATE_B, :, :])
            last.then_inc(mod_ok, 1)
            first_norm(2, 2)
            dve.wait_ge(ld_wn, 16)
            dve.wait_ge(W1_mm, 1)
            for k in range(KD):
                nc.vector.tensor_scalar(W1[:, k, :].rearrange("p (j h) -> p j h", j=W),
                                        ps[:, 4, NK * k:NK * (k + 1)].rearrange("p (h j) -> p j h", j=W),
                                        wn[:, k:k + 1], None, ALU.mult).then_inc(W1_ok, 1)
            dve.wait_ge(sum_mm, NB)
            link(nc.vector.tensor_scalar(var[:, :], sumP, 1.0 / D, EPS_RMS, ALU.mult, ALU.add))
            rsqrt(rms[:, :], var[:, :], 16)
            nc.vector.tensor_scalar(rms[:, :], rms[:, :], SCALE, None, ALU.mult).then_inc(rms_ok, 1)
            dve.wait_ge(W2T_mm, 1)
            for b in range(B):
                for k in range(KD):
                    nc.vector.tensor_scalar(W2T[:, b, k, :].rearrange("p (j h) -> p j h", j=W),
                                            ps[:, 5, NK * k:NK * (k + 1)].rearrange("p (h j) -> p j h", j=W),
                                            mod[:, GATE_A, k, b:b + 1], None, ALU.mult).then_inc(W2T_ok, 1)

            def cut(buf, i):
                return buf.rearrange("p b (j h) -> p b j h", h=HEADS)[:, :, 0:i + 1, :]

            def over(buf, i):
                return buf.unsqueeze(2).broadcast_to([P, B, i + 1, HEADS])

            def subtract_top(i):
                dve.wait_ge(score_mm, i + 1)
                s = cut(ps[:, i % 2, :].rearrange("p (b n) -> p b n", b=B), i)
                link(nc.vector.tensor_reduce(top[:, i % 2, :, :], s.rearrange("p b j h -> p b h j"), AX_X, ALU.max))
                if i >= 2:
                    dve.wait_ge(exp_ok, B * (i - 1))
                nc.vector.tensor_tensor(cut(diff[:, i % 2, :, :], i), s, over(top[:, i % 2, :, :], i),
                                        ALU.subtract).then_inc(diff_ok, 1)

            def divide(i):
                dve.wait_ge(exp_ok, B * (i + 1))
                e = cut(ex[:, i % 2, :, :], i)
                link(nc.vector.tensor_reduce(total[:, i % 2, :, :], e.rearrange("p b j h -> p b h j"), AX_X, ALU.add))
                link(nc.vector.reciprocal(inv[:, i % 2, :, :], total[:, i % 2, :, :]))
                if i >= 2:
                    dve.wait_ge(probT_mm, i - 1)
                nc.vector.tensor_tensor(cut(prob[:, i % 2, :, :], i), e, over(inv[:, i % 2, :, :], i),
                                        ALU.mult).then_inc(prob_ok, 1)

            def add_attention(i):
                dve.wait_ge(att_mm, i + 1)
                f, t = i // 4, i % 4
                rows = x[:, B * f:B * (f + 1), t, :]
                nc.vector.tensor_tensor(rows, ps[:, 4 + i % 2, :].rearrange("p (b d) -> p b d", b=B), rows,
                                        ALU.add).then_inc(x1_ok, 1)
                dve.wait_ge(x1_ok, i + 1)
                for b in range(B):
                    last = tile_stats(B * f + b, t)
                if t == 3:
                    link(last)
                    dve.wait_ge(zT_mm, KD * NB)
                    for tile, ins in normalise(B * f, B):
                        if tile % 4 == 3:
                            ins.then_inc(z2_ok, 1)

            for t in range(W + 2):
                if t < W:
                    subtract_top(t)
                if 1 <= t <= W:
                    divide(t - 1)
                if t >= 2:
                    add_attention(t - 2)

            def hiddens(q, s):
                u = q * (SETS * 4) + 4 * s
                for r in range(4):
                    dve.wait_ge(silu_ok, u + r + 1)
                    dve.wait_ge(up_mm, u + r + 1)
                    nc.vector.tensor_tensor(hid[:, s, r, :], sg[:, r % 2, :], ps[:, 2 + r % 2, :],
                                            ALU.mult).then_inc(hid_ok, 1)

            def keep_two(q, s, first):
                u = q * SETS + s
                a = mag[:, s, :, :]
                dve.wait_ge(mag_ok, 4 * u + 4)
                nc.vector.tensor_tensor(beats[:, 0:3, :], a[:, 0:1, :].broadcast_to([P, 3, T]), a[:, 1:4, :],
                                        ALU.is_ge).then_inc(beats_ok, 1)
                nc.vector.tensor_tensor(beats[:, 3:5, :], a[:, 1:2, :].broadcast_to([P, 2, T]), a[:, 2:4, :],
                                        ALU.is_ge).then_inc(beats_ok, 1)
                nc.vector.tensor_tensor(beats[:, 5, :], a[:, 2, :], a[:, 3, :], ALU.is_ge).then_inc(beats_ok, 1)
                dve.wait_ge(beats_ok, 3 * u + 2)
                nc.vector.tensor_tensor(pairs[:, 0:2, :], beats[:, 1:4:2, :], beats[:, 2:5:2, :],
                                        ALU.add).then_inc(pairs_ok, 1)
                nc.vector.tensor_tensor(pairs[:, 2:4, :], beats[:, 1:3, :], beats[:, 3:5, :],
                                        ALU.add).then_inc(pairs_ok, 1)
                dve.wait_ge(beats_ok, 3 * u + 3)
                dve.wait_ge(pairs_ok, 2 * u + 2)
                nc.vector.tensor_tensor(wins[:, 0, :], pairs[:, 0, :], beats[:, 0, :], ALU.add).then_inc(wins_ok, 1)
                nc.vector.tensor_tensor(wins[:, 1, :], pairs[:, 1, :], beats[:, 0, :], ALU.subtract).then_inc(wins_ok, 1)
                nc.vector.tensor_tensor(wins[:, 2, :], beats[:, 5, :], pairs[:, 2, :], ALU.subtract).then_inc(wins_ok, 1)
                nc.vector.tensor_tensor(wins[:, 3, :], pairs[:, 3, :], beats[:, 5, :], ALU.add).then_inc(wins_ok, 1)
                if not first:
                    dve.wait_ge(down_mm, u - 1)
                for r, (op, bound) in enumerate(((ALU.is_ge, 2.0), (ALU.is_ge, 1.0), (ALU.is_ge, 0.0), (ALU.is_le, 1.0))):
                    dve.wait_ge(wins_ok, 4 * u + r + 1)
                    nc.vector.scalar_tensor_tensor(kept[:, s, r, :], wins[:, r, :], bound, hid[:, s, r, :],
                                                   op, ALU.mult).then_inc(kept_ok, 1)

            def add_ffn(q, turned):
                for m in range(2):
                    dve.wait_ge(back_mm, turned + m + 1)
                    rows = x[:, q, 2 * m:2 * m + 2, :]
                    nc.vector.tensor_tensor(rows, ps[:, 6 + m, :].rearrange("p (t d) -> p t d", t=2), rows,
                                            ALU.add).then_inc(y_ok, 1)

            for s in range(SETS):
                hiddens(0, s)
                keep_two(0, s, True)
            with dve.Fori(1, NB) as q:
                hiddens(q, 0)
                keep_two(q, 0, False)
                hiddens(q, 1)
                keep_two(q, 1, False)
                add_ffn(q - 1, q * 2 - 2)
            add_ffn(NB - 1, 2 * NB - 2)


def kernel(L0_attn_seq, L0_attn_w_norm, L0_attn_w_qkv, L0_attn_w_out, L0_attn_pm, L0_ffn_w_gate, L0_ffn_w_up,
           L0_ffn_w_down, L0_c, L0_wmod):
    import numpy as _np
    import concourse.bacc as _bacc
    from concourse import mybir as _mybir
    from concourse.bass_utils import run_bass_kernel_spmd as _run

    D = L0_attn_seq.shape[2]
    windows = L0_attn_seq.shape[1] // SEGMENT
    heads_in = HEADS * DH

    def memory(m):
        rows = _np.asarray(L0_attn_pm)[m].reshape(HEADS // 2, 2, MEM, DH)[:, :, :windows]
        return rows.transpose(1, 3, 0, 2).reshape(2 * DH, HEADS // 2, windows)

    def grouped(w):
        w = _np.asarray(w)
        return w.reshape(w.shape[0], 2, P, 4).transpose(0, 1, 3, 2)

    laid = {
        "seq": L0_attn_seq,
        "w_norm": L0_attn_w_norm,
        "wqT": _np.asarray(L0_attn_w_qkv)[:, :heads_in].T,
        "w_out": L0_attn_w_out,
        "pmkT": memory(0),
        "pmvT": memory(1),
        "w_gate": grouped(L0_ffn_w_gate),
        "w_up": grouped(L0_ffn_w_up),
        "w_down": L0_ffn_w_down,
        "cT": _np.asarray(L0_c).T,
        "w_mod": L0_wmod,
    }
    nc = _bacc.Bacc("TRN2", target_bir_lowering=False, num_devices=1)
    arrays, args = {}, []
    for name, a in laid.items():
        a = _np.ascontiguousarray(a)
        arrays[f"in_{name}"] = a
        args.append(nc.dram_tensor(f"in_{name}", a.shape, _mybir.dt.from_np(a.dtype), kind="ExternalInput").ap())
    args.append(nc.dram_tensor("out_0", L0_attn_seq.shape, _mybir.dt.float32, kind="ExternalOutput").ap())
    adaln_block(nc, *args)
    return _run(nc, [arrays], core_ids=[0]).results[0]["out_0"]
```

```python
from contextlib import ExitStack

import concourse.bass as bass
from concourse import mybir

ALU = mybir.AluOpType
ACT = mybir.ActivationFunctionType
F32 = mybir.dt.float32
BF16 = mybir.dt.bfloat16
F16 = mybir.dt.float16
I32 = mybir.dt.int32
AX_X = mybir.AxisListType.X
AX_XY = mybir.AxisListType.XY
RMAX = bass.bass_isa.ReduceOp.max

P = 128
HEADS = 32
DH = 64
MEM = 16
SEGMENT = 128
EPS_LN = 1e-5
EPS_RMS = 2.0 ** -23
SHIFT_A, SCALE_A = range(2)
SHIFT_B, SCALE_B, GATE_B = range(3)
RSQRT_SEED = 0x5F3759DF


def adaln_block(nc, seq, w_norm, wqT, w_out, pmkT, pmvT, w_gate, w_up, w_down, cT, w_mod, out):
    B, S, D = seq.shape
    W = S // SEGMENT
    KD = D // P
    HP = HEADS // 2
    PC = HP // 2
    NK = W * HEADS
    SETS = 2
    T = 4 * P
    NB = B * S // T
    HALF = NB // B
    SCALE = float(DH) ** -0.5
    DIAG = P + 2 * W
    assert (D, KD, W, NB, B, HALF) == (256, 2, 8, 4, 2, 2) and S == P * W

    with ExitStack() as ctx:
        def sb(name, shape, dt=F32):
            return ctx.enter_context(nc.sbuf_tensor(name, shape, dt))

        def sem(name):
            return ctx.enter_context(nc.semaphore(name))

        x = sb("x", [P, NB, 4, D])
        rows = sb("rows", [P, NB, 4, D])
        hT = sb("hT", [P, KD, NB, T])
        h2_hi = sb("h2_hi", [P, KD, NB, T], F16)
        h2_lo = sb("h2_lo", [P, KD, NB, T], F16)
        wq_sb = sb("wq_sb", [P, HP, D])
        wo_sb = sb("wo_sb", [P, HP, D])
        wmod_sb = sb("wmod_sb", [P, KD, 6 * D])
        raw = sb("raw", [P, 3, KD * SETS * 4 * P])
        part_hi = sb("part_hi", [P, 3, KD * SETS * 4 * P], F16)
        part_lo = sb("part_lo", [P, 3, KD * SETS * 4 * P], F16)
        pm_sb = sb("pm_sb", [P, 2, HP, W])
        fold = sb("fold", [P, 2, D])
        W1 = sb("W1", [P, KD, NK])
        W2T = sb("W2T", [P, KD, NK])
        W2 = sb("W2", [P, B, 2, D])
        wn = sb("wn", [P, KD])
        c_sb = sb("c_sb", [P, KD, B])
        c_e = sb("c_e", [P, KD, B])
        c_silu = sb("c_silu", [P, KD, B, P])
        mod = sb("mod", [P, 2, B, D])
        modT = sb("modT", [P, 3, KD, B])
        modT_up = sb("modT_up", [P, 2, KD, B])
        gate_a = sb("gate_a", [P, B, D])
        gate_a_parts = sb("gate_a_parts", [P, 2, B, D])
        gate_b = sb("gate_b", [P, KD, B])
        gate_b_parts = sb("gate_b_parts", [P, 2, KD, B])
        y_scale = sb("y_scale", [P, KD, NB])
        ident = sb("ident", [P, P])
        stats = sb("stats", [P, 16, 6])
        mv = sb("mv", [P, 16, 2])
        var = sb("var", [P, 48])
        rstd = sb("rstd", [P, 48])
        newton = sb("newton", [P, 2, 16])
        seed = sb("seed", [P, 16], I32)
        squares = sb("squares", [P, D], BF16)
        sumsq = sb("sumsq", [P, 16])
        top = sb("top", [P, 2, B, HEADS])
        total = sb("total", [P, 2, B, HEADS])
        inv = sb("inv", [P, 2, B, HEADS])
        ex = sb("ex", [P, B * HEADS * (W * (W + 1) // 2)])
        probT = sb("probT", [P, 4, 2, B, P])
        peak = sb("peak", [P, 5])
        peaks_all = sb("peaks_all", [P, 5])
        bound = sb("bound", [P, 5])
        bound_t = sb("bound_t", [P, 3])
        root = sb("root", [P, 1], I32)
        expo = sb("expo", [P, 5], I32)
        up2 = sb("up2", [P, 5])
        down2 = sb("down2", [P, 5])
        un_gate = sb("un_gate", [P, 1])
        un_up = sb("un_up", [P, 1])
        un_y = sb("un_y", [P, 1])
        sg = sb("sg", [P, 2, T])

        def flat(buf, pattern):
            return buf.rearrange(pattern)

        hid = flat(wq_sb[:, :, :], "p a b -> p (a b)").rearrange("p (s r t) -> p s r t", s=2, r=4)
        mag = flat(wo_sb[:, :, :], "p a b -> p (a b)").rearrange("p (s r t) -> p s r t", s=2, r=4)
        down_squares = sg[:, :, :].rearrange("p a t -> p (a t)").bitcast(BF16)
        kept = hT[:, :, :, :]
        kept_hi = raw[:, 0, :].bitcast(F16).rearrange("p (s r t) -> p s r t", s=2, r=4)
        kept_lo = raw[:, 1, :].bitcast(F16).rearrange("p (s r t) -> p s r t", s=2, r=4)
        wins = (gate_a_parts[:, :, :, :].rearrange("p a b d -> p (a b d)").bitcast(BF16)
                .rearrange("p (r t) -> p r t", r=4))
        yT = raw[:, 2, 2 * T:4 * T].rearrange("p (k t) -> p k t", k=KD)
        beats = wmod_sb[:, 0, 0:3 * T].bitcast(BF16).rearrange("p (r t) -> p r t", r=6)
        pairs = wmod_sb[:, 1, 0:2 * T].bitcast(BF16).rearrange("p (r t) -> p r t", r=4)
        pad = [part_hi[:, :, :].rearrange("p a b -> p (a b)")[:, 0:4 * PC * DIAG].bitcast(F32),
               part_lo[:, :, :].rearrange("p a b -> p (a b)")[:, 0:4 * PC * DIAG].bitcast(F32)]

        def weights(part, which):
            if which < 2:
                return part[:, which, :].rearrange("p (k s r g) -> p k s r g", k=KD, s=SETS, r=4)
            return part[:, which, :].rearrange("p (s r d) -> p s r d", s=SETS, r=4)

        wg_hi, wu_hi, wd_hi = (weights(part_hi, w) for w in range(3))
        wg_lo, wu_lo, wd_lo = (weights(part_lo, w) for w in range(3))

        ps = ctx.enter_context(nc.psum_tensor("ps", [P, 8, T], F32))
        modTP = ps[:, 5, 0:3 * KD * B].rearrange("p (m k b) -> p m k b", m=3, k=KD)

        ld_c = sem("ld_c"); ld_modA = sem("ld_modA"); ld_modB = sem("ld_modB")
        ld_x = [sem(f"ld_x{q}") for q in range(NB)]
        ld_pm = sem("ld_pm"); ld_wq = [sem(f"ld_wq{c}") for c in range(2)]; ld_wo = [sem(f"ld_wo{c}") for c in range(2)]
        ld_wn = sem("ld_wn")
        ld_w = [sem(f"ld_w{w}") for w in range(3)]
        zeroed = sem("zeroed"); ident_ok = sem("ident_ok"); pad_ok = sem("pad_ok")
        c_exp = sem("c_exp"); c_ok = sem("c_ok")
        modA_mm = sem("modA_mm"); modA_ok = sem("modA_ok"); modB_mm = sem("modB_mm"); modB_ok = sem("modB_ok")
        gate_step = sem("gate_step"); gate_ok = sem("gate_ok")
        rows_ok = sem("rows_ok"); rows3_ok = sem("rows3_ok"); rows_step = sem("rows_step")
        rowsT_mm = sem("rowsT_mm"); hT_ok = sem("hT_ok"); sumsq_ok = sem("sumsq_ok")
        norms_ok = sem("norms_ok")
        fold_mm = sem("fold_mm"); fold_ok = sem("fold_ok"); foldT_mm = sem("foldT_mm")
        W1_ok = sem("W1_ok"); W2T_ok = sem("W2T_ok"); W2_mm = sem("W2_mm"); W2_ok = sem("W2_ok")
        score_mm = sem("score_mm"); diff_ok = sem("diff_ok"); exp_ok = sem("exp_ok"); prob_ok = sem("prob_ok")
        probT_mm = sem("probT_mm"); probT_ok = sem("probT_ok"); att_mm = sem("att_mm"); x1_ok = sem("x1_ok")
        rows2_first_ok = sem("rows2_first_ok"); h2_first_ok = sem("h2_first_ok")
        rows2_ok = sem("rows2_ok"); rows2T_mm = sem("rows2T_mm"); h2_hi_ok = sem("h2_hi_ok"); h2_ok = sem("h2_ok")
        peak_ok = sem("peak_ok"); peaks_all_ok = sem("peaks_all_ok"); scale_ok = sem("scale_ok")
        y_scale_ok = sem("y_scale_ok")
        w_hi_ok = sem("w_hi_ok"); w_first_ok = sem("w_first_ok"); w_ok = sem("w_ok")
        down_square_ok = sem("down_square_ok"); y_last_ok = sem("y_last_ok")
        gate_mm = sem("gate_mm"); up_mm = sem("up_mm"); silu_ok = sem("silu_ok"); hid_ok = sem("hid_ok")
        mag_ok = sem("mag_ok"); beats_ok = sem("beats_ok"); pairs_ok = sem("pairs_ok"); wins_ok = sem("wins_ok")
        kept_ok = sem("kept_ok"); kept_hi_ok = sem("kept_hi_ok"); kept_lo_ok = sem("kept_lo_ok")
        down_mm = sem("down_mm"); yT_ok = sem("yT_ok"); back_mm = sem("back_mm")
        y_ok = sem("y_ok"); stored = sem("stored"); dve_step = sem("dve_step")

        block = ctx.enter_context(nc.Block())

        def widths(i):
            n = HEADS * (i + 1)
            return [min(P, n)] + ([n - P] if n > P else [])

        def step(i):
            at = B * HEADS * (i * (i + 1) // 2)
            return ex[:, at:at + B * HEADS * (i + 1)].rearrange("p (b n) -> p b n", b=B)

        def att_bank(i):
            return (2 if i < 4 else 6) + i % 2

        def rstd_slot(n):
            return n + 8 * (n // 8)

        def rms_slot(n):
            return 8 + n + 8 * (n // 8)

        def rstd2_slot(n):
            return 32 + n

        PIECES = ((0, 0), (1, 0), (0, 1), (1, 1), (2, 0), (2, 1))

        def piece(buf, n):
            w, s = PIECES[n]
            return weights(buf, w)[:, :, s, :, :] if w < 2 else weights(buf, w)[:, s, :, :]

        def h2_full(q):
            return rows[:, q, :, :].rearrange("p i d -> p (i d)").rearrange("p (k t) -> p k t", k=KD)

        @block.sync
        def _(sp):
            wm = w_mod.rearrange("(k p) n -> p k n", p=P)
            sp.dma_start(c_sb[:, :, :], cT.rearrange("(k p) b -> p k b", p=P)).then_inc(ld_c, 16)
            sp.dma_start(wmod_sb[:, :, 0:2 * D], wm[:, :, 0:2 * D]).then_inc(ld_modA, 16)
            src = seq.rearrange("b (p f i) d -> f b p i d", f=2, i=4)
            sp.dma_start(pm_sb[:, 0, :, :], pmkT).then_inc(ld_pm, 16)
            sp.dma_start(pm_sb[:, 1, :, :], pmvT).then_inc(ld_pm, 16)
            for q in range(B):
                sp.dma_start(x[:, q, :, :], src[q // B, q % B]).then_inc(ld_x[q], 16)
            for c in range(2):
                sp.dma_start(wq_sb[:, PC * c:PC * (c + 1), :],
                             wqT.rearrange("(c g p) d -> c p g d", p=P, c=2)[c]).then_inc(ld_wq[c], 16)
            sp.dma_start(wn[:, :], w_norm.rearrange("(k p) -> p k", p=P),
                         allow_slow_non_contiguous=True).then_inc(ld_wn, 16)
            for q in range(B, NB):
                sp.dma_start(x[:, q, :, :], src[q // B, q % B]).then_inc(ld_x[q], 16)
            sp.dma_start(wmod_sb[:, :, 2 * D:6 * D], wm[:, :, 2 * D:6 * D]).then_inc(ld_modB, 16)
            for c in range(2):
                sp.dma_start(wo_sb[:, PC * c:PC * (c + 1), :],
                             w_out.rearrange("(c g p) d -> c p g d", p=P, c=2)[c]).then_inc(ld_wo[c], 16)
            for w, src in enumerate((w_gate, w_up)):
                sp.dma_start(weights(raw, w), src.rearrange("(k p) s r g -> p k s r g", p=P)).then_inc(ld_w[w], 16)
            sp.dma_start(weights(raw, 2), w_down.rearrange("(s g r) d -> g s r d", s=SETS, r=4)).then_inc(ld_w[2], 16)
            dest = out.rearrange("b (p f i) d -> f b p i d", f=2, i=4)
            for q in range(NB):
                for m in range(2):
                    sp.wait_ge(y_ok, 2 * q + m + 1)
                    sp.dma_start(dest[q // B, q % B][:, 2 * m:2 * m + 2, :], x[:, q, 2 * m:2 * m + 2, :]).then_inc(stored, 16)
            sp.wait_ge(stored, 16 * 2 * NB)

        @block.gpsimd
        def _(pool):
            nc.gpsimd.memset(ident[:, :], 0.0).then_inc(zeroed, 1)
            nc.gpsimd.memset(pad[0], 0.0).then_inc(zeroed, 1)
            nc.gpsimd.memset(pad[1], 0.0).then_inc(zeroed, 1)
            pool.wait_ge(zeroed, 1)
            nc.gpsimd.affine_select(out=ident[:, :], in_=ident[:, :], compare_op=ALU.not_equal, fill=1.0,
                                    base=0, pattern=[[-1, P]], channel_multiplier=1).then_inc(ident_ok, 1)
            pool.wait_ge(zeroed, 3)
            pool.wait_ge(ident_ok, 1)
            pool.wait_ge(ld_pm, 32)
            done = 0
            for m in range(2):
                for r in range(2):
                    if done:
                        pool.wait_ge(pad_ok, done)
                    own = pad[m][DH * r:DH * (r + 1), :].rearrange("p (c g v) -> p c g v", c=2, g=PC)
                    nc.gpsimd.tensor_copy(own[:, :, :, W * r:W * (r + 1)],
                                          pm_sb[DH * r:DH * (r + 1), m, :, :]
                                          .rearrange("p (c g) j -> p c g j", c=2)).then_inc(pad_ok, 1)
                    done += 1
            pool.wait_ge(pad_ok, done)
            gate_steps = [0]

            def gate_link(ins):
                gate_steps[0] += 1
                ins.then_inc(gate_step, 1)
                pool.wait_ge(gate_step, gate_steps[0])

            def head_gate(out, g, parts):
                gate_link(nc.gpsimd.tensor_scalar(parts[1], g, 0.0, 0.5, ALU.is_ge, ALU.subtract))
                gate_link(nc.gpsimd.tensor_tensor(parts[0], g, parts[1], ALU.mult))
                gate_link(nc.gpsimd.tensor_scalar(parts[0], parts[0], 0.125, 4.0, ALU.max, ALU.mult))
                return nc.gpsimd.tensor_tensor(out, parts[0], parts[1], ALU.mult)

            def normalise(q, slot):
                for t in range(4):
                    m, n = 4 * q + t, slot(4 * q + t)
                    last = nc.gpsimd.tensor_scalar(rows[:, q, t, :], x[:, q, t, :], mv[:, m, 0:1], rstd[:, n:n + 1],
                                                   ALU.subtract, ALU.mult)
                return last

            def split_weight(n):
                pool.wait_ge(w_hi_ok, n + 1)
                nc.gpsimd.tensor_tensor(piece(part_lo, n), piece(raw, n), piece(part_hi, n),
                                        ALU.subtract).then_inc(w_ok, 1)

            def split_h2(q):
                for k in range(KD):
                    pool.wait_ge(h2_hi_ok, KD * q + k + 1)
                    nc.gpsimd.tensor_tensor(h2_lo[:, k, q, :], h2_full(q)[:, k, :], h2_hi[:, k, q, :],
                                            ALU.subtract).then_inc(h2_ok, 1)

            def split_kept(unit, s, r):
                pool.wait_ge(kept_hi_ok, unit * 4 + (r + 1))
                nc.gpsimd.tensor_tensor(kept_lo[:, s, r, :], kept[:, s, r, :], kept_hi[:, s, r, :],
                                        ALU.subtract).then_inc(kept_lo_ok, 1)

            pool.wait_ge(norms_ok, 2)
            pool.wait_ge(modA_ok, 1)
            every = [P, 4, D]
            normalise(3, rstd_slot).then_inc(rows_step, 1)
            pool.wait_ge(rows_step, 1)
            nc.gpsimd.tensor_tensor(rows[:, 3, :, :], rows[:, 3, :, :],
                                    mod[:, SCALE_A, 3 % B:3 % B + 1, :].broadcast_to(every), ALU.mult).then_inc(rows_step, 1)
            pool.wait_ge(rows_step, 2)
            nc.gpsimd.tensor_tensor(rows[:, 3, :, :], rows[:, 3, :, :],
                                    mod[:, SHIFT_A, 3 % B:3 % B + 1, :].broadcast_to(every), ALU.add).then_inc(rows3_ok, 1)

            pool.wait_ge(modB_ok, 2)
            head_gate(gate_a[:, :, :], gate_a[:, :, :], [gate_a_parts[:, n, :, :] for n in range(2)]).then_inc(gate_ok, 1)
            gate_link(head_gate(gate_b[:, :, :], modT[:, GATE_B, :, :], [gate_b_parts[:, n, :, :] for n in range(2)]))
            pool.wait_ge(peak_ok, 4)
            pool.wait_ge(down_square_ok, 1)
            nc.gpsimd.partition_all_reduce(peaks_all[:, :], peak[:, :], P, RMAX).then_inc(peaks_all_ok, 1)
            pool.wait_ge(scale_ok, 1)
            for f in range(NB // B):
                last = nc.gpsimd.tensor_scalar(y_scale[:, :, B * f:B * (f + 1)], gate_b[:, :, :],
                                               un_y[:, 0:1], None, ALU.mult)
                last.then_inc(y_scale_ok, 1)
            pool.wait_ge(norms_ok, 4)
            pool.wait_ge(rowsT_mm, KD * NB)
            pool.wait_ge(sumsq_ok, 4 * NB)
            normalise(1, rstd2_slot).then_inc(rows2_ok, 1)
            split_weight(2)
            split_weight(3)
            split_h2(1)
            split_weight(4)
            split_weight(5)
            for r in range(4):
                split_kept(0, 0, r)
            pool.wait_ge(norms_ok, 5)
            for q in (2, 3):
                normalise(q, rstd2_slot).then_inc(rows2_ok, 1)
            for r in range(4):
                split_kept(1, 1, r)
            split_h2(2)
            split_h2(3)
            with pool.Fori(1, NB) as q:
                for s in range(SETS):
                    for r in range(4):
                        split_kept(q * SETS + s, s, r)

        @block.scalar
        def _(act):
            act.wait_ge(ld_c, 16)
            nc.scalar.activation(c_e[:, :, :], c_sb[:, :, :], ACT.Exp, scale=-1.0).then_inc(c_exp, 1)
            act.wait_ge(modA_mm, 1)
            nc.scalar.activation(mod[:, SHIFT_A, :, :], ps[:, 0:B, 0:D], ACT.Copy)
            nc.scalar.activation(mod[:, SCALE_A, :, :], ps[:, 0:B, D:2 * D], ACT.Copy, bias=1.0).then_inc(modA_ok, 1)

            def sum_squares(q):
                if q < 3:
                    act.wait_ge(rows_ok, q + 1)
                else:
                    act.wait_ge(rows3_ok, 1)
                for t in range(4):
                    if q or t:
                        act.wait_ge(sumsq_ok, 4 * q + t)
                    nc.scalar.activation(squares[:, :], rows[:, q, t, :], ACT.Square,
                                         accum_out=sumsq[:, 4 * q + t:4 * q + t + 1]).then_inc(sumsq_ok, 1)

            def take_hT(q):
                for k in range(KD):
                    act.wait_ge(rowsT_mm, KD * q + k + 1)
                    nc.scalar.activation(hT[:, k, q, :], ps[:, 6 + k, :], ACT.Copy).then_inc(hT_ok, 1)

            def take_fold(m):
                act.wait_ge(fold_mm, m + 1)
                if m:
                    act.wait_ge(foldT_mm, m)
                nc.scalar.activation(fold[:, :, :], ps[:, 2, :].rearrange("p (c d) -> p c d", c=2),
                                     ACT.Copy).then_inc(fold_ok, 1)

            def exps(i):
                act.wait_ge(diff_ok, i + 1)
                if i % 4 == 0:
                    act.wait_ge(norms_ok, 2 + i // 4)
                for b in range(B):
                    n = rms_slot(4 * (B * (i // 4) + b) + i % 4)
                    nc.scalar.activation(step(i)[:, b, :], step(i)[:, b, :], ACT.Exp,
                                         scale=rstd[:, n:n + 1]).then_inc(exp_ok, 1)

            def take_probT(i):
                act.wait_ge(probT_mm, i + 1)
                if i >= 4:
                    act.wait_ge(att_mm, i - 3)
                for c, w in enumerate(widths(i)):
                    last = nc.scalar.activation(probT[0:w, i % 4, c, :, :],
                                                ps[0:w, 4 + i % 2, 2 * P * c:2 * P * (c + 1)]
                                                .rearrange("p (b t) -> p b t", b=B), ACT.Copy)
                last.then_inc(probT_ok, 1)

            def split_weight(n):
                if n == 0:
                    act.wait_ge(scale_ok, 1)
                    act.wait_ge(foldT_mm, 2)
                w = PIECES[n][0]
                last = nc.scalar.activation(piece(part_hi, n), piece(raw, n), ACT.Copy, scale=up2[:, 1 + w:2 + w])
                if n >= 2:
                    last = nc.scalar.activation(piece(raw, n), piece(raw, n), ACT.Copy, scale=up2[:, 1 + w:2 + w])
                last.then_inc(w_hi_ok, 1)

            def take_h2(q):
                b = q % B
                act.wait_ge(rows2T_mm, KD * (q + 1))
                for k in range(KD):
                    for out in (h2_hi[:, k, q, :], h2_full(q)[:, k, :]):
                        last = nc.scalar.activation(out, ps[:, 6 + k, :], ACT.Identity,
                                                    scale=modT_up[:, SCALE_B, k, b:b + 1],
                                                    bias=modT_up[:, SHIFT_B, k, b:b + 1])
                    last.then_inc(h2_hi_ok, 1)

            sum_squares(0)
            sum_squares(1)
            take_fold(0)
            take_hT(0)
            take_hT(1)
            act.wait_ge(modB_mm, 1)
            nc.scalar.activation(gate_a[:, :, :], ps[:, 4, :].rearrange("p (b d) -> p b d", b=B), ACT.Copy).then_inc(modB_ok, 1)
            nc.scalar.activation(modT[:, 0:3:2, :, :], modTP[:, 0:3:2, :, :], ACT.Copy)
            nc.scalar.activation(modT[:, SCALE_B, :, :], modTP[:, SCALE_B, :, :], ACT.Copy, bias=1.0).then_inc(modB_ok, 1)
            exps(0)
            sum_squares(2)
            exps(1)
            take_probT(0)
            take_hT(2)
            exps(2)
            take_probT(1)
            sum_squares(3)
            exps(3)
            take_probT(2)
            take_hT(3)
            act.wait_ge(ld_w[2], 16)
            nc.scalar.activation(down_squares, raw[:, 2, :], ACT.Square, accum_out=peak[:, 4:5]).then_inc(down_square_ok, 1)
            take_probT(3)
            take_fold(1)
            act.wait_ge(foldT_mm, 2)
            nc.scalar.activation(W2T[:, :, :].rearrange("p k (j h) -> p k j h", j=W),
                                 ps[:, 3, :].rearrange("p (k h j) -> p k j h", k=KD, j=W), ACT.Copy).then_inc(W2T_ok, 1)
            exps(4)
            exps(5)
            split_weight(0)
            split_weight(1)
            exps(6)
            take_h2(0)
            exps(7)
            split_weight(2)
            split_weight(3)

            def keep_part(unit, s, r, first):
                act.wait_ge(kept_ok, unit * 4 + r + 1)
                if not first and r == 0:
                    act.wait_ge(down_mm, unit - 1)
                nc.scalar.activation(kept_hi[:, s, r, :], kept[:, s, r, :], ACT.Copy).then_inc(kept_hi_ok, 1)

            def silus(q, s, nth, extra):
                u = q * (SETS * 4) + 4 * s

                def after(r):
                    if r in extra:
                        extra[r]()

                def silu(r):
                    act.wait_ge(gate_mm, u + r + 1)
                    if nth or r >= 2:
                        act.wait_ge(hid_ok, u + r - 1)
                    nc.scalar.activation(sg[:, r % 2, :], ps[:, r % 2, :], ACT.Silu,
                                         scale=un_gate[:, 0:1]).then_inc(silu_ok, 1)

                def magnitude(r):
                    act.wait_ge(hid_ok, u + r + 1)
                    nc.scalar.activation(mag[:, s, r, :], hid[:, s, r, :], ACT.Abs).then_inc(mag_ok, 1)

                if nth:
                    before = q * SETS + s - 1
                    keep_part(before, 1 - s, 0, nth < 3)
                    keep_part(before, 1 - s, 1, nth < 3)
                silu(0)
                if nth:
                    keep_part(before, 1 - s, 2, nth < 3)
                    keep_part(before, 1 - s, 3, nth < 3)
                silu(1)
                if nth >= 2:
                    act.wait_ge(beats_ok, q * (3 * SETS) + 3 * (s - 1))
                magnitude(0)
                after(0)
                silu(2)
                magnitude(1)
                after(1)
                magnitude(2)
                silu(3)
                after(2)
                magnitude(3)
                after(3)

            def take_y(q):
                act.wait_ge(down_mm, SETS * q + SETS)
                for k in range(KD):
                    nc.scalar.activation(yT[:, k, :], ps[:, 4 + k, :], ACT.Identity,
                                         scale=y_scale[:, k, bass.ds(q, 1)]).then_inc(yT_ok, 1)

            silus(0, 0, 0, {0: lambda: (take_probT(4), take_h2(1)), 1: lambda: take_probT(5),
                            2: lambda: (take_probT(6), split_weight(4)), 3: lambda: split_weight(5)})
            silus(0, 1, 1, {0: lambda: take_probT(7)})
            silus(1, 0, 2, {1: lambda: take_h2(2), 3: lambda: take_h2(3)})
            act.wait_ge(y_scale_ok, 2)
            act.wait_ge(w_ok, 4)
            take_y(0)
            silus(1, 1, 3, {})
            with act.Fori(2, NB) as q:
                silus(q, 0, 3, {})
                take_y(q - 1)
                silus(q, 1, 3, {})
            for r in range(4):
                keep_part(NB * SETS - 1, 1, r, False)
            act.wait_ge(down_mm, SETS * NB)
            nc.scalar.activation(yT[:, 0, :], ps[:, 4, :], ACT.Identity, scale=y_scale[:, 0, NB - 1:NB]).then_inc(yT_ok, 1)

        @block.tensor
        def _(pe):
            pe.wait_ge(c_ok, 1)
            pe.wait_ge(ld_modA, 16)
            for b in range(B):
                for k in range(KD):
                    last = nc.tensor.matmul(ps[:, b, :], c_silu[:, k, b, :], wmod_sb[:, k, 0:2 * D],
                                            start=(k == 0), stop=(k == KD - 1))
            last.then_inc(modA_mm, 1)

            def product(w, m, arrived, chunks=(0, 1)):
                for c in chunks:
                    pe.wait_ge(arrived[c], 16)
                    for g in range(PC):
                        at = DIAG * PC * c + P * g
                        last = nc.tensor.matmul(ps[:, 2, D * c:D * (c + 1)], pad[m][:, at:at + P],
                                                w[:, PC * c + g, :], start=(g == 0), stop=(g == PC - 1))
                if chunks[-1] == 1:
                    last.then_inc(fold_mm, 1)

            def product_turned(m):
                pe.wait_ge(fold_ok, m + 1)
                if m:
                    pe.wait_ge(W1_ok, KD)
                for k in range(KD):
                    for c in range(2):
                        last = nc.tensor.transpose(ps[:, 3, NK * k + P * c:NK * k + P * (c + 1)],
                                                   fold[:, c, P * k:P * (k + 1)], ident[:, :])
                last.then_inc(foldT_mm, 1)

            def turn_rows(q):
                if q < 3:
                    pe.wait_ge(rows_ok, q + 1)
                else:
                    pe.wait_ge(rows3_ok, 1)
                for k in range(KD):
                    if q >= 1:
                        pe.wait_ge(hT_ok, KD * (q - 1) + k + 1)
                    for t in range(4):
                        last = nc.tensor.transpose(ps[:, 6 + k, P * t:P * (t + 1)],
                                                   rows[:, q, t, P * k:P * (k + 1)], ident[:, :])
                    last.then_inc(rowsT_mm, 1)

            def modulation_b():
                pe.wait_ge(ld_modB, 16)
                for b in range(B):
                    for k in range(KD):
                        nc.tensor.matmul(ps[:, 4, D * b:D * (b + 1)], c_silu[:, k, b, :], wmod_sb[:, k, 2 * D:3 * D],
                                         start=(k == 0), stop=(k == KD - 1))
                for m in range(3):
                    for n in range(KD):
                        at = (3 + m) * D + P * n
                        for k in range(KD):
                            last = nc.tensor.matmul(modTP[:, m, n, :], wmod_sb[:, k, at:at + P], c_silu[:, k, :, 0],
                                                    start=(k == 0), stop=(k == KD - 1))
                last.then_inc(modB_mm, 1)

            def scores(i):
                n = HEADS * (i + 1)
                if i >= 2:
                    pe.wait_ge(diff_ok, i - 1)
                if i == 4:
                    pe.wait_ge(hT_ok, KD * NB)
                for b in range(B):
                    q = B * (i // 4) + b
                    for k in range(KD):
                        last = nc.tensor.matmul(ps[:, i % 2, D * b:D * b + n], hT[:, k, q, P * (i % 4):P * (i % 4 + 1)],
                                                W1[:, k, 0:n], start=(k == 0), stop=(k == KD - 1))
                last.then_inc(score_mm, 1)

            def turn_probs(i):
                pe.wait_ge(prob_ok, i + 1)
                if i >= 2:
                    pe.wait_ge(probT_ok, i - 1)
                for c, w in enumerate(widths(i)):
                    for b in range(B):
                        last = nc.tensor.transpose(ps[0:w, 4 + i % 2, P * (2 * c + b):P * (2 * c + b + 1)],
                                                   step(i)[:, b, P * c:P * c + w], ident[:, :])
                last.then_inc(probT_mm, 1)

            def attend(i):
                pe.wait_ge(probT_ok, i + 1)
                if i in (2, 3, 6, 7):
                    pe.wait_ge(x1_ok, i - 1)
                ws = widths(i)
                for b in range(B):
                    for c, w in enumerate(ws):
                        last = nc.tensor.matmul(ps[:, att_bank(i), D * b:D * (b + 1)], probT[0:w, i % 4, c, b, :],
                                                W2[0:w, b, c, :], start=(c == 0), stop=(c == len(ws) - 1))
                last.then_inc(att_mm, 1)

            def turn_rows2(q):
                if q == 0:
                    pe.wait_ge(rows2_first_ok, 1)
                else:
                    pe.wait_ge(rows2_ok, q)
                if q == 2:
                    pe.wait_ge(x1_ok, W)
                for k in range(KD):
                    if q == 0:
                        pe.wait_ge(hT_ok, KD * (NB - 1) + k + 1)
                    elif q != 2:
                        pe.wait_ge(h2_hi_ok, KD * (q - 1) + k + 1)
                    for t in range(4):
                        last = nc.tensor.transpose(ps[:, 6 + k, P * t:P * (t + 1)],
                                                   rows[:, q, t, P * k:P * (k + 1)], ident[:, :])
                    last.then_inc(rows2T_mm, 1)

            pe.wait_ge(ident_ok, 1)
            pe.wait_ge(pad_ok, 2)
            product(wq_sb, 0, ld_wq)
            turn_rows(0)
            product_turned(0)
            turn_rows(1)
            modulation_b()
            pe.wait_ge(W1_ok, KD)
            pe.wait_ge(modA_ok, 1)
            pe.wait_ge(hT_ok, KD * B)
            scores(0)
            scores(1)
            pe.wait_ge(pad_ok, 4)
            product(wo_sb, 1, ld_wo, [0])
            turn_rows(2)
            pe.wait_ge(modB_ok, 2)
            turn_probs(0)
            scores(2)
            turn_probs(1)
            scores(3)
            turn_rows(3)
            turn_probs(2)
            product(wo_sb, 1, ld_wo, [1])
            turn_probs(3)
            product_turned(1)
            scores(4)
            pe.wait_ge(W2T_ok, 1)
            for c in range(2):
                for k in range(KD):
                    last = nc.tensor.transpose(ps[:, 2, D * c + P * k:D * c + P * (k + 1)],
                                               W2T[:, k, P * c:P * (c + 1)], ident[:, :])
            last.then_inc(W2_mm, 1)
            scores(5)
            pe.wait_ge(W2_ok, B)
            attend(0)
            attend(1)
            scores(6)
            attend(2)
            attend(3)
            scores(7)
            turn_rows2(0)

            pe.wait_ge(diff_ok, W)
            pe.wait_ge(x1_ok, 4)

            def gate_up(q, s, nth, extra):
                u = q * (SETS * 4) + 4 * s
                for r in range(4):
                    for hi, lo, bank, read, done in ((wg_hi, wg_lo, r % 2, silu_ok, gate_mm),
                                                     (wu_hi, wu_lo, 2 + r % 2, hid_ok, up_mm)):
                        if nth or r >= 2:
                            pe.wait_ge(read, u + r - 1)
                        for k in range(KD):
                            nc.tensor.matmul(ps[:, bank, :], lo[:, k, s, r, :], h2_hi[:, k, q, :],
                                             start=(k == 0), stop=False)
                            nc.tensor.matmul(ps[:, bank, :], hi[:, k, s, r, :], h2_lo[:, k, q, :],
                                             start=False, stop=False)
                            last = nc.tensor.matmul(ps[:, bank, :], hi[:, k, s, r, :], h2_hi[:, k, q, :],
                                                    start=False, stop=(k == KD - 1))
                        last.then_inc(done, 1)
                    if r in extra:
                        extra[r]()

            def down(unit, s):
                for r in range(4):
                    pe.wait_ge(kept_lo_ok, unit * 4 + r + 1)
                    for k in range(KD):
                        cols = slice(P * k, P * (k + 1))
                        nc.tensor.matmul(ps[:, 4 + k, :], wd_lo[:, s, r, cols], kept_hi[:, s, r, :],
                                         start=(s == 0 and r == 0), stop=False)
                        nc.tensor.matmul(ps[:, 4 + k, :], wd_hi[:, s, r, cols], kept_lo[:, s, r, :],
                                         start=False, stop=False)
                        last = nc.tensor.matmul(ps[:, 4 + k, :], wd_hi[:, s, r, cols], kept_hi[:, s, r, :],
                                                start=False, stop=(s == SETS - 1 and r == 3))
                last.then_inc(down_mm, 1)

            def turn_y(yT_count):
                pe.wait_ge(yT_ok, yT_count)
                for t in range(4):
                    for k in range(KD):
                        last = nc.tensor.transpose(ps[:, 6 + t // 2, D * (t % 2) + P * k:D * (t % 2) + P * (k + 1)],
                                                   yT[:, k, P * t:P * (t + 1)], ident[:, :])
                    if t % 2:
                        last.then_inc(back_mm, 1)

            pe.wait_ge(h2_first_ok, KD)
            pe.wait_ge(w_first_ok, 2)
            gate_up(0, 0, 0, {0: lambda: (turn_probs(4), turn_rows2(1)), 1: lambda: turn_probs(5),
                              2: lambda: (pe.wait_ge(h2_hi_ok, KD * 2), attend(4), turn_probs(6)),
                              3: lambda: attend(5)})
            pe.wait_ge(w_ok, 2)
            gate_up(0, 1, 1, {0: lambda: (attend(6), turn_probs(7)), 1: lambda: attend(7)})
            pe.wait_ge(probT_ok, W)
            pe.wait_ge(w_ok, 4)
            down(0, 0)
            pe.wait_ge(h2_ok, KD)
            gate_up(1, 0, 1, {1: lambda: turn_rows2(2), 3: lambda: turn_rows2(3)})
            down(1, 1)
            gate_up(1, 1, 1, {})
            pe.wait_ge(yT_ok, KD)
            down(2, 0)
            pe.wait_ge(h2_hi_ok, KD * NB)
            turn_y(KD)
            pe.wait_ge(h2_ok, KD * (NB - 1))
            with pe.Fori(2, NB) as q:
                gate_up(q, 0, 1, {})
                down(q * SETS - 1, 1)
                gate_up(q, 1, 1, {})
                pe.wait_ge(yT_ok, q * KD)
                down(q * SETS, 0)
                turn_y(q * KD)
            down(NB * SETS - 1, 1)
            pe.wait_ge(y_ok, 2 * (NB - 1))
            pe.wait_ge(y_last_ok, 1)
            turn_y(NB * KD - 1)

        @block.vector
        def _(dve):
            steps = [0]

            def link(ins):
                steps[0] += 1
                ins.then_inc(dve_step, 1)
                dve.wait_ge(dve_step, steps[0])

            def rsqrt(dst, src, n):
                bits, half, yy = seed[:, 0:n], newton[:, 0, 0:n], newton[:, 1, 0:n]
                link(nc.vector.tensor_scalar(bits, src.bitcast(I32), 1, None, ALU.arith_shift_right))
                nc.vector.tensor_scalar(half, src, -0.5, None, ALU.mult)
                link(nc.vector.tensor_scalar(dst.bitcast(I32), bits, -1.0, float(RSQRT_SEED), ALU.mult, ALU.add))
                for n in range(3):
                    link(nc.vector.tensor_tensor(yy, dst, dst, ALU.mult))
                    link(nc.vector.tensor_tensor(yy, yy, half, ALU.mult))
                    last = nc.vector.scalar_tensor_tensor(dst, yy, 1.5, dst, ALU.add, ALU.mult)
                    if n < 2:
                        link(last)
                return last

            def tile_stats(q, t):
                return nc.vector.bn_stats(stats[:, 4 * q + t, :], x[:, q, t, :])

            def variance(q0, nq, slot):
                a, b = 4 * q0, 4 * (q0 + nq)
                for t in range(a, b):
                    last = nc.vector.bn_aggr(mv[:, t, :], stats[:, t, :])
                link(last)
                n = slot(a)
                return nc.vector.tensor_scalar(var[:, n:n + b - a], mv[:, a:b, 1], EPS_LN, None, ALU.add)

            def mean_square(half):
                dve.wait_ge(sumsq_ok, 8 * (half + 1))
                n = rms_slot(8 * half)
                return nc.vector.tensor_scalar(var[:, n:n + 8], sumsq[:, 8 * half:8 * half + 8], 1.0 / D, EPS_RMS,
                                               ALU.mult, ALU.add)

            def norms(a, b):
                rsqrt(rstd[:, a:b], var[:, a:b], b - a).then_inc(norms_ok, 1)

            def modulate(q):
                for t in range(4):
                    n = 4 * q + t
                    last = nc.vector.scalar_tensor_tensor(rows[:, q, t, :], x[:, q, t, :], mv[:, n, 0:1],
                                                          mod[:, SCALE_A, q % B, :], ALU.subtract, ALU.mult)
                link(last)
                for t in range(4):
                    n = rstd_slot(4 * q + t)
                    last = nc.vector.scalar_tensor_tensor(rows[:, q, t, :], rows[:, q, t, :], rstd[:, n:n + 1],
                                                          mod[:, SHIFT_A, q % B, :], ALU.mult, ALU.add)
                last.then_inc(rows_ok, 1)

            def normalise_first():
                dve.wait_ge(rowsT_mm, KD)
                dve.wait_ge(sumsq_ok, 4)
                for t in range(4):
                    n = rstd2_slot(t)
                    last = nc.vector.tensor_scalar(rows[:, 0, t, :], x[:, 0, t, :], mv[:, t, 0:1], rstd[:, n:n + 1],
                                                   ALU.subtract, ALU.mult)
                last.then_inc(rows2_first_ok, 1)

            dve.wait_ge(c_exp, 1)
            link(nc.vector.tensor_scalar(c_e[:, :, :], c_e[:, :, :], 1.0, None, ALU.add))
            link(nc.vector.reciprocal(c_e[:, :, :], c_e[:, :, :]))
            every = [P, KD, B, P]
            nc.vector.tensor_tensor(c_silu[:, :, :, :], c_sb[:, :, :].unsqueeze(3).broadcast_to(every),
                                    c_e[:, :, :].unsqueeze(3).broadcast_to(every), ALU.mult).then_inc(c_ok, 1)

            def row_stats(half):
                for q in range(B * half, B * (half + 1)):
                    dve.wait_ge(ld_x[q], 16)
                    for t in range(4):
                        last = tile_stats(q, t)
                link(last)
                return variance(B * half, B, rstd_slot)

            def scale_W1():
                dve.wait_ge(ld_wn, 16)
                dve.wait_ge(foldT_mm, 1)
                for k in range(KD):
                    nc.vector.tensor_scalar(W1[:, k, :].rearrange("p (j h) -> p j h", j=W),
                                            ps[:, 3, NK * k:NK * (k + 1)].rearrange("p (h j) -> p j h", j=W),
                                            wn[:, k:k + 1], SCALE, ALU.mult, ALU.mult).then_inc(W1_ok, 1)

            def gate_W2():
                dve.wait_ge(W2_mm, 1)
                dve.wait_ge(gate_ok, 1)
                for b in range(B):
                    nc.vector.tensor_tensor(W2[:, b, :, :], ps[:, 2, :].rearrange("p (c d) -> p c d", c=2),
                                            gate_a[:, b:b + 1, :].broadcast_to([P, 2, D]), ALU.mult).then_inc(W2_ok, 1)

            def peaks(w):
                dve.wait_ge(ld_w[w], 16)
                nc.vector.tensor_reduce(peak[:, 2 + w:3 + w], raw[:, w, :], AX_X, ALU.max,
                                        apply_absolute_value=True).then_inc(peak_ok, 1)

            def bounds():
                dve.wait_ge(peaks_all_ok, 1)
                s, a, m_gate, m_up = (peaks_all[:, n:n + 1] for n in range(4))
                nc.vector.scalar_tensor_tensor(bound[:, 0:1], a, 16.0, s, ALU.mult, ALU.add)
                nc.vector.tensor_copy(bound[:, 1:3], peaks_all[:, 2:4])
                nc.vector.tensor_scalar(root[:, :], peaks_all[:, 4:5].bitcast(I32), 1, None, ALU.arith_shift_right)
                nc.vector.tensor_tensor(bound_t[:, 2:3], m_gate, m_up, ALU.mult)
                link(nc.vector.tensor_tensor(bound_t[:, 0:1], a, s, ALU.add))
                nc.vector.tensor_scalar(bound[:, 3:4].bitcast(I32), root[:, :], float(127 << 22), None, ALU.add)
                link(nc.vector.scalar_tensor_tensor(bound_t[:, 1:2], bound_t[:, 0:1], 65536.0, bound_t[:, 0:1],
                                                    ALU.mult, ALU.mult))
                link(nc.vector.tensor_tensor(bound[:, 4:5], bound_t[:, 1:2], bound_t[:, 2:3], ALU.mult))
                link(nc.vector.tensor_scalar(expo[:, :], bound[:, :].bitcast(I32), 0x7F800000, None, ALU.bitwise_and))
                link(nc.vector.tensor_scalar(expo[:, :], expo[:, :], float(64 << 23), None, ALU.max))
                link(nc.vector.tensor_scalar(up2[:, :].bitcast(I32), expo[:, :], -1.0, float(268 << 23), ALU.mult, ALU.add))
                nc.vector.tensor_scalar(modT_up[:, :, :, :], modT[:, SHIFT_B:SCALE_B + 1, :, :], up2[:, 0:1], None, ALU.mult)
                link(nc.vector.tensor_scalar(down2[:, :].bitcast(I32), expo[:, :], float(14 << 23), None, ALU.subtract))
                link(nc.vector.tensor_tensor(un_up[:, :], down2[:, 0:1], down2[:, 2:3], ALU.mult))
                nc.vector.tensor_tensor(un_gate[:, :], down2[:, 0:1], down2[:, 1:2], ALU.mult)
                nc.vector.tensor_tensor(un_y[:, :], down2[:, 3:4], down2[:, 4:5], ALU.mult)
                nc.vector.tensor_tensor(un_up[:, :], un_up[:, :], up2[:, 4:5], ALU.mult).then_inc(scale_ok, 1)
                dve.wait_ge(scale_ok, 1)

            def split_weight(n):
                dve.wait_ge(w_hi_ok, n + 1)
                w = PIECES[n][0]
                nc.vector.scalar_tensor_tensor(piece(part_lo, n), piece(raw, n), up2[:, 1 + w:2 + w],
                                               piece(part_hi, n), ALU.mult, ALU.subtract).then_inc(w_first_ok, 1)

            def cut(buf):
                return buf.rearrange("p b (j h) -> p b j h", h=HEADS)

            def over(buf, i):
                return buf.unsqueeze(2).broadcast_to([P, B, i + 1, HEADS])

            def subtract_top(i):
                dve.wait_ge(score_mm, i + 1)
                s = cut(ps[:, i % 2, :].rearrange("p (b n) -> p b n", b=B)[:, :, 0:HEADS * (i + 1)])
                link(nc.vector.tensor_reduce(top[:, i % 2, :, :], s.rearrange("p b j h -> p b h j"), AX_X, ALU.max))
                nc.vector.tensor_tensor(cut(step(i)), s, over(top[:, i % 2, :, :], i), ALU.subtract).then_inc(diff_ok, 1)

            def divide(i):
                dve.wait_ge(exp_ok, B * (i + 1))
                e = cut(step(i))
                link(nc.vector.tensor_reduce(total[:, i % 2, :, :], e.rearrange("p b j h -> p b h j"), AX_X, ALU.add))
                link(nc.vector.reciprocal(inv[:, i % 2, :, :], total[:, i % 2, :, :]))
                nc.vector.tensor_tensor(e, e, over(inv[:, i % 2, :, :], i), ALU.mult).then_inc(prob_ok, 1)

            def add_attention(i):
                dve.wait_ge(att_mm, i + 1)
                f, t = i // 4, i % 4
                old = x[:, B * f:B * (f + 1), t, :]
                nc.vector.tensor_tensor(old, ps[:, att_bank(i), :].rearrange("p (b d) -> p b d", b=B), old,
                                        ALU.add).then_inc(x1_ok, 1)
                dve.wait_ge(x1_ok, i + 1)
                for b in range(B):
                    last = tile_stats(B * f + b, t)
                if t == 3:
                    link(last)
                    link(variance(B * f, B, rstd2_slot))
                    norms(rstd2_slot(8 * f), rstd2_slot(8 * f) + 8)
                    dve.wait_ge(norms_ok, 4 + f)

            def split_h2_first():
                for k in range(KD):
                    dve.wait_ge(h2_hi_ok, k + 1)
                    nc.vector.tensor_tensor(h2_lo[:, k, 0, :], h2_full(0)[:, k, :], h2_hi[:, k, 0, :],
                                            ALU.subtract).then_inc(h2_first_ok, 1)

            link(row_stats(0))
            norms(0, 8)
            dve.wait_ge(norms_ok, 1)
            dve.wait_ge(modA_ok, 1)
            modulate(0)
            modulate(1)
            row_stats(1)
            link(mean_square(0))
            norms(8, 24)
            dve.wait_ge(norms_ok, 2)
            scale_W1()
            modulate(2)
            subtract_top(0)
            subtract_top(1)
            divide(0)
            dve.wait_ge(modB_ok, 2)
            for m in (SHIFT_B, SCALE_B):
                nc.vector.tensor_reduce(peak[:, m:m + 1], modT[:, m, :, :], AX_XY, ALU.max,
                                        apply_absolute_value=True).then_inc(peak_ok, 1)
            subtract_top(2)
            divide(1)
            subtract_top(3)
            divide(2)
            peaks(0)
            divide(3)
            link(mean_square(1))
            norms(24, 32)
            peaks(1)
            subtract_top(4)
            gate_W2()
            bounds()
            subtract_top(5)
            add_attention(0)
            subtract_top(6)
            add_attention(1)
            add_attention(2)
            add_attention(3)
            normalise_first()
            subtract_top(7)
            split_weight(0)
            split_h2_first()
            split_weight(1)
            divide(4)

            def hiddens(q, s, nth, extra):
                unit = q * SETS + s
                a = mag[:, s, :, :]

                def sum_beats():
                    dve.wait_ge(beats_ok, unit * 3 + 2)
                    nc.vector.tensor_tensor(pairs[:, 0, :], beats[:, 0, :], beats[:, 1, :], ALU.add).then_inc(pairs_ok, 1)
                    nc.vector.tensor_tensor(pairs[:, 1, :], beats[:, 2, :], beats[:, 0, :], ALU.subtract).then_inc(pairs_ok, 1)
                    nc.vector.tensor_tensor(pairs[:, 2, :], beats[:, 1, :], beats[:, 2, :], ALU.add).then_inc(pairs_ok, 1)

                for r in range(4):
                    dve.wait_ge(silu_ok, unit * 4 + r + 1)
                    dve.wait_ge(up_mm, unit * 4 + r + 1)
                    nc.vector.scalar_tensor_tensor(hid[:, s, r, :], sg[:, r % 2, :], un_up[:, 0:1], ps[:, 2 + r % 2, :],
                                                   ALU.mult, ALU.mult).then_inc(hid_ok, 1)
                    if r in extra:
                        extra[r]()
                    if r == 0:
                        continue
                    if r == 3:
                        sum_beats()
                    dve.wait_ge(mag_ok, unit * 4 + r + 1)
                    first = r * (r - 1) // 2
                    nc.vector.tensor_tensor(beats[:, first:first + r, :], a[:, 0:r, :],
                                            a[:, r:r + 1, :].broadcast_to([P, r, T]), ALU.is_ge).then_inc(beats_ok, 1)
                dve.wait_ge(beats_ok, unit * 3 + 3)
                dve.wait_ge(pairs_ok, unit * 4 + 3)
                nc.vector.tensor_tensor(wins[:, 0:2, :], pairs[:, 0:2, :], beats[:, 3:5, :], ALU.add).then_inc(wins_ok, 1)
                nc.vector.tensor_tensor(pairs[:, 3, :], beats[:, 3, :], beats[:, 4, :], ALU.add).then_inc(pairs_ok, 1)
                nc.vector.tensor_tensor(wins[:, 2, :], beats[:, 5, :], pairs[:, 2, :], ALU.subtract).then_inc(wins_ok, 1)
                if nth:
                    dve.wait_ge(kept_lo_ok, 4 * unit - 4)
                for r, (op, limit) in enumerate(((ALU.is_ge, 2.0), (ALU.is_ge, 1.0), (ALU.is_ge, 0.0), (ALU.is_le, 1.0))):
                    if r == 3:
                        dve.wait_ge(pairs_ok, unit * 4 + 4)
                        nc.vector.tensor_tensor(wins[:, 3, :], pairs[:, 3, :], beats[:, 5, :], ALU.add).then_inc(wins_ok, 1)
                    dve.wait_ge(wins_ok, unit * 3 + (1, 1, 2, 3)[r])
                    nc.vector.scalar_tensor_tensor(kept[:, s, r, :], wins[:, r, :], limit, hid[:, s, r, :],
                                                   op, ALU.mult).then_inc(kept_ok, 1)

            def add_ffn(q):
                for m in range(2):
                    dve.wait_ge(back_mm, q * 2 + m + 1)
                    old = x[:, q, 2 * m:2 * m + 2, :]
                    nc.vector.tensor_tensor(old, ps[:, 6 + m, :].rearrange("p (t d) -> p t d", t=2), old,
                                            ALU.add).then_inc(y_ok, 1)

            hiddens(0, 0, 0, {0: lambda: divide(5), 1: lambda: divide(6), 2: lambda: divide(7),
                              3: lambda: add_attention(4)})
            add_attention(5)
            hiddens(0, 1, 0, {1: lambda: add_attention(6), 2: lambda: add_attention(7)})
            hiddens(1, 0, 1, {})
            hiddens(1, 1, 1, {})
            add_ffn(0)
            with dve.Fori(2, NB) as q:
                hiddens(q, 0, 1, {})
                hiddens(q, 1, 1, {})
                add_ffn(q - 1)
            dve.wait_ge(down_mm, SETS * NB)
            nc.vector.tensor_scalar(yT[:, 1, :], ps[:, 5, :], y_scale[:, 1, NB - 1:NB], None, ALU.mult).then_inc(y_last_ok, 1)
            add_ffn(NB - 1)


def kernel(L0_attn_seq, L0_attn_w_norm, L0_attn_w_qkv, L0_attn_w_out, L0_attn_pm, L0_ffn_w_gate, L0_ffn_w_up,
           L0_ffn_w_down, L0_c, L0_wmod):
    import numpy as _np
    import concourse.bacc as _bacc
    from concourse import mybir as _mybir
    from concourse.bass_utils import run_bass_kernel_spmd as _run

    D = L0_attn_seq.shape[2]
    windows = L0_attn_seq.shape[1] // SEGMENT
    heads_in = HEADS * DH

    def memory(m):
        rows = _np.asarray(L0_attn_pm)[m].reshape(HEADS // 2, 2, MEM, DH)[:, :, :windows]
        return rows.transpose(1, 3, 0, 2).reshape(2 * DH, HEADS // 2, windows)

    def grouped(w):
        w = _np.asarray(w)
        return w.reshape(w.shape[0], 2, P, 4).transpose(0, 1, 3, 2)

    laid = {
        "seq": L0_attn_seq,
        "w_norm": L0_attn_w_norm,
        "wqT": _np.asarray(L0_attn_w_qkv)[:, :heads_in].T,
        "w_out": L0_attn_w_out,
        "pmkT": memory(0),
        "pmvT": memory(1),
        "w_gate": grouped(L0_ffn_w_gate),
        "w_up": grouped(L0_ffn_w_up),
        "w_down": L0_ffn_w_down,
        "cT": _np.asarray(L0_c).T,
        "w_mod": L0_wmod,
    }
    nc = _bacc.Bacc("TRN2", target_bir_lowering=False, num_devices=1)
    arrays, args = {}, []
    for name, a in laid.items():
        a = _np.ascontiguousarray(a)
        arrays[f"in_{name}"] = a
        args.append(nc.dram_tensor(f"in_{name}", a.shape, _mybir.dt.from_np(a.dtype), kind="ExternalInput").ap())
    args.append(nc.dram_tensor("out_0", L0_attn_seq.shape, _mybir.dt.float32, kind="ExternalOutput").ap())
    adaln_block(nc, *args)
    return _run(nc, [arrays], core_ids=[0]).results[0]["out_0"]
```

```python
from contextlib import ExitStack

import concourse.bass as bass
from concourse import mybir

ALU = mybir.AluOpType
ACT = mybir.ActivationFunctionType
F32 = mybir.dt.float32
BF16 = mybir.dt.bfloat16
F16 = mybir.dt.float16
I32 = mybir.dt.int32
AX_X = mybir.AxisListType.X
AX_XY = mybir.AxisListType.XY
RMAX = bass.bass_isa.ReduceOp.max

P = 128
HEADS = 32
DH = 64
MEM = 16
SEGMENT = 128
EPS_LN = 1e-5
EPS_RMS = 2.0 ** -23
SHIFT_A, SCALE_A = range(2)
SHIFT_B, SCALE_B, GATE_B = range(3)
RSQRT_SEED = 0x5F3759DF


def adaln_block(nc, seq, w_norm, wqT, w_out, pmkT, pmvT, w_gate, w_up, w_down, cT, w_mod, out):
    B, S, D = seq.shape
    W = S // SEGMENT
    KD = D // P
    HP = HEADS // 2
    PC = HP // 2
    NK = W * HEADS
    SETS = 2
    T = 4 * P
    NB = B * S // T
    HALF = NB // B
    SCALE = float(DH) ** -0.5
    DIAG = P + 2 * W
    assert (D, KD, W, NB, B, HALF) == (256, 2, 8, 4, 2, 2) and S == P * W

    with ExitStack() as ctx:
        def sb(name, shape, dt=F32):
            return ctx.enter_context(nc.sbuf_tensor(name, shape, dt))

        def sem(name):
            return ctx.enter_context(nc.semaphore(name))

        x = sb("x", [P, NB, 4, D])
        rows = sb("rows", [P, NB, 4, D])
        hT = sb("hT", [P, KD, NB, T])
        h2_hi = sb("h2_hi", [P, KD, NB, T], F16)
        h2_lo = sb("h2_lo", [P, KD, NB, T], F16)
        wq_sb = sb("wq_sb", [P, HP, D])
        wo_sb = sb("wo_sb", [P, HP, D])
        wmod_sb = sb("wmod_sb", [P, KD, 6 * D])
        raw = sb("raw", [P, 3, KD * SETS * 4 * P])
        part_hi = sb("part_hi", [P, 3, KD * SETS * 4 * P], F16)
        part_lo = sb("part_lo", [P, 3, KD * SETS * 4 * P], F16)
        pm_sb = sb("pm_sb", [P, 2, HP, W])
        fold = sb("fold", [P, 2, D])
        W1 = sb("W1", [P, KD, NK])
        W2T = sb("W2T", [P, KD, NK])
        W2 = sb("W2", [P, B, 2, D])
        wn = sb("wn", [P, KD])
        c_sb = sb("c_sb", [P, KD, B])
        c_e = sb("c_e", [P, KD, B])
        c_silu = sb("c_silu", [P, KD, B, P])
        mod = sb("mod", [P, 2, B, D])
        modT = sb("modT", [P, 3, KD, B])
        modT_up = sb("modT_up", [P, 2, KD, B])
        gate_a = sb("gate_a", [P, B, D])
        gate_a_parts = sb("gate_a_parts", [P, 2, B, D])
        gate_b = sb("gate_b", [P, KD, B])
        gate_b_parts = sb("gate_b_parts", [P, 2, KD, B])
        y_scale = sb("y_scale", [P, KD, NB])
        ident = sb("ident", [P, P])
        stats = sb("stats", [P, 16, 6])
        mv = sb("mv", [P, 16, 2])
        var = sb("var", [P, 48])
        rstd = sb("rstd", [P, 48])
        newton = sb("newton", [P, 2, 16])
        seed = sb("seed", [P, 16], I32)
        shifted = sb("shifted", [P, 16])
        squares = sb("squares", [P, D], BF16)
        sumsq = sb("sumsq", [P, 16])
        top = sb("top", [P, 4, B, HEADS])
        total = sb("total", [P, 4, B, HEADS])
        inv = sb("inv", [P, 4, B, HEADS])
        ex = sb("ex", [P, B * HEADS * (W * (W + 1) // 2)])
        probT = sb("probT", [P, 4, 2, B, P])
        peak = sb("peak", [P, 5])
        peaks_all = sb("peaks_all", [P, 5])
        bound = sb("bound", [P, 5])
        bound_t = sb("bound_t", [P, 3])
        root = sb("root", [P, 1], I32)
        expo = sb("expo", [P, 5], I32)
        up2 = sb("up2", [P, 5])
        down2 = sb("down2", [P, 5])
        un_gate = sb("un_gate", [P, 1])
        un_up = sb("un_up", [P, 1])
        un_y = sb("un_y", [P, 1])
        sg = sb("sg", [P, 2, T])

        def flat(buf, pattern):
            return buf.rearrange(pattern)

        hid = flat(wq_sb[:, :, :], "p a b -> p (a b)").rearrange("p (s r t) -> p s r t", s=2, r=4)
        mag = flat(wo_sb[:, :, :], "p a b -> p (a b)").rearrange("p (s r t) -> p s r t", s=2, r=4)
        down_squares = sg[:, :, :].rearrange("p a t -> p (a t)").bitcast(BF16)
        kept = hT[:, :, :, :]
        kept_hi = raw[:, 0, :].bitcast(F16).rearrange("p (s r t) -> p s r t", s=2, r=4)
        kept_lo = raw[:, 1, :].bitcast(F16).rearrange("p (s r t) -> p s r t", s=2, r=4)
        wins = (gate_a_parts[:, :, :, :].rearrange("p a b d -> p (a b d)").bitcast(BF16)
                .rearrange("p (r t) -> p r t", r=4))
        yT = raw[:, 2, 2 * T:4 * T].rearrange("p (k t) -> p k t", k=KD)
        beats = wmod_sb[:, 0, 0:3 * T].bitcast(BF16).rearrange("p (r t) -> p r t", r=6)
        pairs = wmod_sb[:, 1, 0:2 * T].bitcast(BF16).rearrange("p (r t) -> p r t", r=4)
        pad = [part_hi[:, :, :].rearrange("p a b -> p (a b)")[:, 0:4 * PC * DIAG].bitcast(F32),
               part_lo[:, :, :].rearrange("p a b -> p (a b)")[:, 0:4 * PC * DIAG].bitcast(F32)]

        def weights(part, which):
            if which < 2:
                return part[:, which, :].rearrange("p (k s r g) -> p k s r g", k=KD, s=SETS, r=4)
            return part[:, which, :].rearrange("p (s r d) -> p s r d", s=SETS, r=4)

        wg_hi, wu_hi, wd_hi = (weights(part_hi, w) for w in range(3))
        wg_lo, wu_lo, wd_lo = (weights(part_lo, w) for w in range(3))

        ps = ctx.enter_context(nc.psum_tensor("ps", [P, 8, T], F32))
        modTP = ps[:, 5, 0:3 * KD * B].rearrange("p (m k b) -> p m k b", m=3, k=KD)

        ld_c = sem("ld_c"); ld_modA = sem("ld_modA"); ld_modB = sem("ld_modB")
        ld_x = [sem(f"ld_x{q}") for q in range(NB)]
        ld_pm = sem("ld_pm"); ld_wq = [sem(f"ld_wq{c}") for c in range(2)]; ld_wo = [sem(f"ld_wo{c}") for c in range(2)]
        ld_wn = sem("ld_wn")
        ld_w = [sem(f"ld_w{w}") for w in range(3)]
        zeroed = sem("zeroed"); ident_ok = sem("ident_ok"); pad_ok = sem("pad_ok")
        c_exp = sem("c_exp"); c_ok = sem("c_ok")
        modA_mm = sem("modA_mm"); modA_ok = sem("modA_ok"); modB_mm = sem("modB_mm"); modB_ok = sem("modB_ok")
        gate_step = sem("gate_step"); gate_ok = sem("gate_ok")
        rows_ok = sem("rows_ok"); rowsT_mm = sem("rowsT_mm"); hT_ok = sem("hT_ok"); sumsq_ok = sem("sumsq_ok")
        norms_ok = sem("norms_ok")
        fold_mm = sem("fold_mm"); fold_ok = sem("fold_ok"); foldT_mm = sem("foldT_mm")
        W1_ok = sem("W1_ok"); W2T_ok = sem("W2T_ok"); W2_mm = sem("W2_mm"); W2_raw_ok = sem("W2_raw_ok"); W2_ok = sem("W2_ok")
        score_mm = sem("score_mm"); diff_ok = sem("diff_ok"); exp_ok = sem("exp_ok"); prob_ok = sem("prob_ok"); inv_ok = sem("inv_ok")
        probT_mm = sem("probT_mm"); probT_ok = sem("probT_ok"); att_mm = sem("att_mm")
        x1_ok = sem("x1_ok"); x1_first_ok = sem("x1_first_ok"); scaled_ok = sem("scaled_ok"); stats_ok = sem("stats_ok")
        rows2_half_ok = sem("rows2_half_ok"); h2_first_ok = sem("h2_first_ok")
        rows2_ok = sem("rows2_ok"); rows2T_mm = sem("rows2T_mm"); h2_hi_ok = sem("h2_hi_ok"); h2_full_ok = sem("h2_full_ok"); h2_ok = sem("h2_ok")
        peak_ok = sem("peak_ok"); peaks_all_ok = sem("peaks_all_ok"); scale_ok = sem("scale_ok")
        y_scale_ok = sem("y_scale_ok")
        w_hi_ok = sem("w_hi_ok"); w_first_ok = sem("w_first_ok"); w_ok = sem("w_ok")
        down_square_ok = sem("down_square_ok"); y_last_ok = sem("y_last_ok")
        gate_mm = sem("gate_mm"); up_mm = sem("up_mm"); silu_ok = sem("silu_ok"); hid_ok = sem("hid_ok")
        mag_ok = sem("mag_ok"); beats_ok = sem("beats_ok"); pairs_ok = sem("pairs_ok"); wins_ok = sem("wins_ok")
        kept_ok = sem("kept_ok"); kept_hi_ok = sem("kept_hi_ok"); kept_lo_ok = sem("kept_lo_ok")
        down_mm = sem("down_mm"); yT_ok = sem("yT_ok"); back_mm = sem("back_mm")
        y_ok = sem("y_ok"); stored = sem("stored"); dve_step = sem("dve_step")

        block = ctx.enter_context(nc.Block())

        def widths(i):
            n = HEADS * (i + 1)
            return [min(P, n)] + ([n - P] if n > P else [])

        def step(i):
            at = B * HEADS * (i * (i + 1) // 2)
            return ex[:, at:at + B * HEADS * (i + 1)].rearrange("p (b n) -> p b n", b=B)

        def att_bank(i):
            return 2 + i if i < 4 else 6 + i % 2

        BY_POOL = (6, 7)

        def cut(buf):
            return buf.rearrange("p b (j h) -> p b j h", h=HEADS)

        def over(buf, i):
            return buf.unsqueeze(2).broadcast_to([P, B, i + 1, HEADS])

        BY_PE = (0, 1, 2, 3)

        def score_place(i):
            n = HEADS * (i + 1)
            if i < 4:
                two = ps[:, i // 2, D * (i % 2):D * (i % 2 + 1)]
                return two.rearrange("p (b n) -> p b n", b=B)[:, :, 0:n]
            return ps[:, i % 2, :].rearrange("p (b n) -> p b n", b=B)[:, :, 0:n]

        def probT_place(i, c):
            w = widths(i)[c]
            if i < 4:
                return ps[0:w, 4 + i // 2, B * P * (i % 2):B * P * (i % 2 + 1)]
            return ps[0:w, 4 + i % 2, B * P * c:B * P * (c + 1)]

        def rstd_slot(n):
            return n + 8 * (n // 8)

        def rms_slot(n):
            return 8 + n + 8 * (n // 8)

        def rstd2_slot(n):
            return 32 + n

        PIECES = ((0, 0), (1, 0), (0, 1), (1, 1), (2, 0), (2, 1))

        BY_DVE = (0, 1, 3)

        def piece(buf, n):
            w, s = PIECES[n]
            return weights(buf, w)[:, :, s, :, :] if w < 2 else weights(buf, w)[:, s, :, :]

        def h2_full(q):
            return rows[:, q, :, :].rearrange("p i d -> p (i d)").rearrange("p (k t) -> p k t", k=KD)

        @block.sync
        def _(sp):
            wm = w_mod.rearrange("(k p) n -> p k n", p=P)
            sp.dma_start(c_sb[:, :, :], cT.rearrange("(k p) b -> p k b", p=P)).then_inc(ld_c, 16)
            sp.dma_start(wmod_sb[:, :, 0:2 * D], wm[:, :, 0:2 * D]).then_inc(ld_modA, 16)
            src = seq.rearrange("b (p f i) d -> f b p i d", f=2, i=4)
            sp.dma_start(pm_sb[:, 0, :, :], pmkT).then_inc(ld_pm, 16)
            sp.dma_start(pm_sb[:, 1, :, :], pmvT).then_inc(ld_pm, 16)
            for q in range(B):
                sp.dma_start(x[:, q, :, :], src[q // B, q % B]).then_inc(ld_x[q], 16)
            for c in range(2):
                sp.dma_start(wq_sb[:, PC * c:PC * (c + 1), :],
                             wqT.rearrange("(c g p) d -> c p g d", p=P, c=2)[c]).then_inc(ld_wq[c], 16)
            sp.dma_start(wn[:, :], w_norm.rearrange("(k p) -> p k", p=P),
                         allow_slow_non_contiguous=True).then_inc(ld_wn, 16)
            sp.dma_start(wmod_sb[:, :, 2 * D:6 * D], wm[:, :, 2 * D:6 * D]).then_inc(ld_modB, 16)
            for q in range(B, NB):
                sp.dma_start(x[:, q, :, :], src[q // B, q % B]).then_inc(ld_x[q], 16)
            for c in range(2):
                sp.dma_start(wo_sb[:, PC * c:PC * (c + 1), :],
                             w_out.rearrange("(c g p) d -> c p g d", p=P, c=2)[c]).then_inc(ld_wo[c], 16)
            for w, src in enumerate((w_gate, w_up)):
                sp.dma_start(weights(raw, w), src.rearrange("(k p) s r g -> p k s r g", p=P)).then_inc(ld_w[w], 16)
            sp.dma_start(weights(raw, 2), w_down.rearrange("(s g r) d -> g s r d", s=SETS, r=4)).then_inc(ld_w[2], 16)
            dest = out.rearrange("b (p f i) d -> f b p i d", f=2, i=4)
            for q in range(NB):
                for m in range(2):
                    sp.wait_ge(y_ok, 2 * q + m + 1)
                    sp.dma_start(dest[q // B, q % B][:, 2 * m:2 * m + 2, :], x[:, q, 2 * m:2 * m + 2, :]).then_inc(stored, 16)
            sp.wait_ge(stored, 16 * 2 * NB)

        @block.gpsimd
        def _(pool):
            nc.gpsimd.memset(ident[:, :], 0.0).then_inc(zeroed, 1)
            nc.gpsimd.memset(pad[0], 0.0).then_inc(zeroed, 1)
            nc.gpsimd.memset(pad[1], 0.0).then_inc(zeroed, 1)
            pool.wait_ge(zeroed, 1)
            nc.gpsimd.affine_select(out=ident[:, :], in_=ident[:, :], compare_op=ALU.not_equal, fill=1.0,
                                    base=0, pattern=[[-1, P]], channel_multiplier=1).then_inc(ident_ok, 1)
            pool.wait_ge(zeroed, 3)
            pool.wait_ge(ident_ok, 1)
            pool.wait_ge(ld_pm, 32)
            done = 0
            for m in range(2):
                for r in range(2):
                    if done:
                        pool.wait_ge(pad_ok, done)
                    own = pad[m][DH * r:DH * (r + 1), :].rearrange("p (c g v) -> p c g v", c=2, g=PC)
                    nc.gpsimd.tensor_copy(own[:, :, :, W * r:W * (r + 1)],
                                          pm_sb[DH * r:DH * (r + 1), m, :, :]
                                          .rearrange("p (c g) j -> p c g j", c=2)).then_inc(pad_ok, 1)
                    done += 1
            pool.wait_ge(pad_ok, done)
            gate_steps = [0]

            def gate_link(ins):
                gate_steps[0] += 1
                ins.then_inc(gate_step, 1)
                pool.wait_ge(gate_step, gate_steps[0])

            def head_gate(out, g, parts):
                gate_link(nc.gpsimd.tensor_scalar(parts[1], g, 0.0, 0.5, ALU.is_ge, ALU.subtract))
                gate_link(nc.gpsimd.tensor_tensor(parts[0], g, parts[1], ALU.mult))
                gate_link(nc.gpsimd.tensor_scalar(parts[0], parts[0], 0.125, 4.0, ALU.max, ALU.mult))
                return nc.gpsimd.tensor_tensor(out, parts[0], parts[1], ALU.mult)

            def split_weight(n):
                pool.wait_ge(w_hi_ok, n + 1)
                nc.gpsimd.tensor_tensor(piece(part_lo, n), piece(raw, n), piece(part_hi, n),
                                        ALU.subtract).then_inc(w_ok, 1)

            def divide(nth, i):
                pool.wait_ge(inv_ok, nth + 1)
                nc.gpsimd.tensor_tensor(cut(step(i)), cut(step(i)), over(inv[:, i % 4, :, :], i),
                                        ALU.mult).then_inc(prob_ok, 1)

            def split_h2(q):
                for k in range(KD):
                    pool.wait_ge(h2_full_ok, KD * q + k + 1)
                    nc.gpsimd.tensor_tensor(h2_lo[:, k, q, :], h2_full(q)[:, k, :], h2_hi[:, k, q, :],
                                            ALU.subtract).then_inc(h2_ok, 1)

            def split_kept(unit, s, r):
                pool.wait_ge(kept_hi_ok, unit * 4 + (r + 1))
                nc.gpsimd.tensor_tensor(kept_lo[:, s, r, :], kept[:, s, r, :], kept_hi[:, s, r, :],
                                        ALU.subtract).then_inc(kept_lo_ok, 1)

            pool.wait_ge(modB_ok, 2)
            head_gate(gate_a[:, :, :], gate_a[:, :, :], [gate_a_parts[:, n, :, :] for n in range(2)]).then_inc(gate_ok, 1)
            last = head_gate(gate_b[:, :, :], modT[:, GATE_B, :, :], [gate_b_parts[:, n, :, :] for n in range(2)])
            gate_link(last)
            pool.wait_ge(gate_ok, 1)
            pool.wait_ge(W2_raw_ok, 1)
            for b in range(B):
                nc.gpsimd.tensor_tensor(W2[:, b, :, :], fold[:, :, :],
                                        gate_a[:, b:b + 1, :].broadcast_to([P, 2, D]), ALU.mult).then_inc(W2_ok, 1)
            pool.wait_ge(peak_ok, 4)
            pool.wait_ge(down_square_ok, 1)
            nc.gpsimd.partition_all_reduce(peaks_all[:, :], peak[:, :], P, RMAX).then_inc(peaks_all_ok, 1)
            pool.wait_ge(scale_ok, 1)
            for f in range(NB // B):
                last = nc.gpsimd.tensor_scalar(y_scale[:, :, B * f:B * (f + 1)], gate_b[:, :, :],
                                               un_y[:, 0:1], None, ALU.mult)
                last.then_inc(y_scale_ok, 1)
            split_weight(2)
            for nth, i in enumerate(BY_POOL):
                divide(nth, i)
            split_h2(1)
            split_weight(4)
            split_weight(5)
            for r in range(4):
                split_kept(0, 0, r)
            for r in range(4):
                split_kept(1, 1, r)
            for r in range(4):
                split_kept(2, 0, r)
            split_h2(2)
            split_h2(3)
            for r in range(4):
                split_kept(3, 1, r)
            with pool.Fori(2, NB) as q:
                for s in range(SETS):
                    for r in range(4):
                        split_kept(q * SETS + s, s, r)

        @block.scalar
        def _(act):
            act.wait_ge(ld_c, 16)
            nc.scalar.activation(c_e[:, :, :], c_sb[:, :, :], ACT.Exp, scale=-1.0).then_inc(c_exp, 1)
            act.wait_ge(modA_mm, 1)
            nc.scalar.activation(mod[:, SHIFT_A, :, :], ps[:, 0:B, 0:D], ACT.Copy)
            nc.scalar.activation(mod[:, SCALE_A, :, :], ps[:, 0:B, D:2 * D], ACT.Copy, bias=1.0).then_inc(modA_ok, 1)

            def sum_squares(q):
                act.wait_ge(rows_ok, q + 1)
                for t in range(4):
                    if q or t:
                        act.wait_ge(sumsq_ok, 4 * q + t)
                    nc.scalar.activation(squares[:, :], rows[:, q, t, :], ACT.Square,
                                         accum_out=sumsq[:, 4 * q + t:4 * q + t + 1]).then_inc(sumsq_ok, 1)

            def take_hT(q):
                for k in range(KD):
                    act.wait_ge(rowsT_mm, KD * q + k + 1)
                    nc.scalar.activation(hT[:, k, q, :], ps[:, 6 + k, :], ACT.Copy).then_inc(hT_ok, 1)

            def take_fold(m):
                act.wait_ge(fold_mm, m + 1)
                if m:
                    act.wait_ge(foldT_mm, m)
                nc.scalar.activation(fold[:, :, :], ps[:, 2, :].rearrange("p (c d) -> p c d", c=2),
                                     ACT.Copy).then_inc(fold_ok, 1)

            def exps(i):
                act.wait_ge(diff_ok, i + 1)
                if i % 4 == 0:
                    act.wait_ge(norms_ok, 2 + i // 4)
                for b in range(B):
                    n = rms_slot(4 * (B * (i // 4) + b) + i % 4)
                    nc.scalar.activation(step(i)[:, b, :], step(i)[:, b, :], ACT.Exp,
                                         scale=rstd[:, n:n + 1]).then_inc(exp_ok, 1)

            def take_probT(i):
                act.wait_ge(probT_mm, i + 1 if i >= 4 else 2 * (i // 2) + 2)
                if i >= 4:
                    act.wait_ge(att_mm, i - 3)
                for c, w in enumerate(widths(i)):
                    last = nc.scalar.activation(probT[0:w, i % 4, c, :, :],
                                                probT_place(i, c).rearrange("p (b t) -> p b t", b=B), ACT.Copy)
                last.then_inc(probT_ok, 1)

            def split_weight(n):
                if n == 0:
                    act.wait_ge(scale_ok, 1)
                    act.wait_ge(foldT_mm, 2)
                w = PIECES[n][0]
                last = nc.scalar.activation(piece(part_hi, n), piece(raw, n), ACT.Copy, scale=up2[:, 1 + w:2 + w])
                if n not in BY_DVE:
                    last = nc.scalar.activation(piece(raw, n), piece(raw, n), ACT.Copy, scale=up2[:, 1 + w:2 + w])
                last.then_inc(w_hi_ok, 1)

            def take_x1(i):
                act.wait_ge(att_mm, i + 1)
                nc.scalar.activation(x[:, 0:B, i, :], ps[:, att_bank(i), :].rearrange("p (b d) -> p b d", b=B),
                                     ACT.Copy).then_inc(x1_first_ok, 1)

            def normalise(q, tiles=range(4)):
                act.wait_ge(norms_ok, 4 + q // B)
                act.wait_ge(rowsT_mm, KD * (q + 1))
                for t in tiles:
                    m, n = 4 * q + t, rstd2_slot(4 * q + t)
                    last = nc.scalar.activation(rows[:, q, t, :], x[:, q, t, :], ACT.Identity, scale=rstd[:, n:n + 1],
                                                bias=shifted[:, m:m + 1])
                last.then_inc(rows2_ok, 1)

            def take_h2(q):
                b = q % B
                act.wait_ge(rows2T_mm, KD * (q + 1))
                for which, done in ((h2_hi[:, :, q, :], h2_hi_ok), (h2_full(q), h2_full_ok)):
                    for k in range(KD):
                        nc.scalar.activation(which[:, k, :], ps[:, 6 + k, :], ACT.Identity,
                                             scale=modT_up[:, SCALE_B, k, b:b + 1],
                                             bias=modT_up[:, SHIFT_B, k, b:b + 1]).then_inc(done, 1)

            sum_squares(0)
            sum_squares(1)
            take_fold(0)
            take_hT(0)
            take_hT(1)
            exps(0)
            exps(1)
            exps(2)
            exps(3)
            act.wait_ge(modB_mm, 1)
            nc.scalar.activation(gate_a[:, :, :], ps[:, 4, :].rearrange("p (b d) -> p b d", b=B), ACT.Copy).then_inc(modB_ok, 1)
            nc.scalar.activation(modT[:, 0:3:2, :, :], modTP[:, 0:3:2, :, :], ACT.Copy)
            nc.scalar.activation(modT[:, SCALE_B, :, :], modTP[:, SCALE_B, :, :], ACT.Copy, bias=1.0).then_inc(modB_ok, 1)
            sum_squares(2)
            act.wait_ge(ld_w[2], 16)
            nc.scalar.activation(down_squares, raw[:, 2, :], ACT.Square, accum_out=peak[:, 4:5]).then_inc(down_square_ok, 1)
            take_fold(1)
            take_hT(2)
            act.wait_ge(foldT_mm, 2)
            nc.scalar.activation(W2T[:, :, :].rearrange("p k (j h) -> p k j h", j=W),
                                 ps[:, 3, :].rearrange("p (k h j) -> p k j h", k=KD, j=W), ACT.Copy).then_inc(W2T_ok, 1)
            take_hT(3)
            act.wait_ge(W2_mm, 1)
            nc.scalar.activation(fold[:, :, :], ps[:, 2, :].rearrange("p (c d) -> p c d", c=2), ACT.Copy).then_inc(W2_raw_ok, 1)
            for i in range(4):
                take_probT(i)
            sum_squares(3)
            take_x1(0)
            take_x1(1)
            exps(4)
            take_x1(2)
            split_weight(0)
            take_x1(3)
            split_weight(1)
            exps(5)
            split_weight(2)
            normalise(0, (0, 1))
            exps(6)
            take_h2(0)
            exps(7)

            def keep_part(unit, s, r, first):
                act.wait_ge(kept_ok, unit * 4 + r + 1)
                if not first and r == 0:
                    act.wait_ge(down_mm, unit - 1)
                nc.scalar.activation(kept_hi[:, s, r, :], kept[:, s, r, :], ACT.Copy).then_inc(kept_hi_ok, 1)

            def silus(q, s, nth, extra):
                u = q * (SETS * 4) + 4 * s

                def after(r):
                    if r in extra:
                        extra[r]()

                def silu(r):
                    act.wait_ge(gate_mm, u + r + 1)
                    if nth or r >= 2:
                        act.wait_ge(hid_ok, u + r - 1)
                    nc.scalar.activation(sg[:, r % 2, :], ps[:, r % 2, :], ACT.Silu,
                                         scale=un_gate[:, 0:1]).then_inc(silu_ok, 1)

                def magnitude(r):
                    act.wait_ge(hid_ok, u + r + 1)
                    nc.scalar.activation(mag[:, s, r, :], hid[:, s, r, :], ACT.Abs).then_inc(mag_ok, 1)

                if nth:
                    before = q * SETS + s - 1
                    keep_part(before, 1 - s, 0, nth < 3)
                    keep_part(before, 1 - s, 1, nth < 3)
                silu(0)
                if nth:
                    keep_part(before, 1 - s, 2, nth < 3)
                    keep_part(before, 1 - s, 3, nth < 3)
                silu(1)
                if nth >= 2:
                    act.wait_ge(beats_ok, q * (5 * SETS) + 5 * (s - 1))
                magnitude(0)
                after(0)
                silu(2)
                magnitude(1)
                after(1)
                magnitude(2)
                silu(3)
                after(2)
                magnitude(3)
                after(3)

            def take_y(q):
                act.wait_ge(down_mm, SETS * q + SETS)
                for k in range(KD):
                    nc.scalar.activation(yT[:, k, :], ps[:, 4 + k, :], ACT.Identity,
                                         scale=y_scale[:, k, bass.ds(q, 1)]).then_inc(yT_ok, 1)

            silus(0, 0, 0, {0: lambda: normalise(1), 1: lambda: (split_weight(3), take_probT(4)),
                            2: lambda: (take_h2(1), take_probT(5)), 3: lambda: take_probT(6)})
            split_weight(4)
            split_weight(5)
            silus(0, 1, 1, {0: lambda: take_probT(7)})
            silus(1, 0, 2, {1: lambda: normalise(2), 2: lambda: normalise(3), 3: lambda: take_h2(2)})
            act.wait_ge(y_scale_ok, 2)
            act.wait_ge(w_ok, 3)
            take_y(0)
            silus(1, 1, 3, {1: lambda: take_h2(3)})
            with act.Fori(2, NB) as q:
                silus(q, 0, 3, {})
                take_y(q - 1)
                silus(q, 1, 3, {})
            for r in range(4):
                keep_part(NB * SETS - 1, 1, r, False)
            act.wait_ge(down_mm, SETS * NB)
            nc.scalar.activation(yT[:, 0, :], ps[:, 4, :], ACT.Identity, scale=y_scale[:, 0, NB - 1:NB]).then_inc(yT_ok, 1)

        @block.tensor
        def _(pe):
            pe.wait_ge(c_ok, 1)
            pe.wait_ge(ld_modA, 16)
            for b in range(B):
                for k in range(KD):
                    last = nc.tensor.matmul(ps[:, b, :], c_silu[:, k, b, :], wmod_sb[:, k, 0:2 * D],
                                            start=(k == 0), stop=(k == KD - 1))
            last.then_inc(modA_mm, 1)

            def product(w, m, arrived):
                for c in range(2):
                    pe.wait_ge(arrived[c], 16)
                    for g in range(PC):
                        at = DIAG * PC * c + P * g
                        last = nc.tensor.matmul(ps[:, 2, D * c:D * (c + 1)], pad[m][:, at:at + P],
                                                w[:, PC * c + g, :], start=(g == 0), stop=(g == PC - 1))
                last.then_inc(fold_mm, 1)

            def product_turned(m):
                pe.wait_ge(fold_ok, m + 1)
                if m:
                    pe.wait_ge(W1_ok, KD)
                for k in range(KD):
                    for c in range(2):
                        last = nc.tensor.transpose(ps[:, 3, NK * k + P * c:NK * k + P * (c + 1)],
                                                   fold[:, c, P * k:P * (k + 1)], ident[:, :])
                last.then_inc(foldT_mm, 1)

            def turn_rows(q):
                pe.wait_ge(rows_ok, q + 1)
                for k in range(KD):
                    if q >= 1:
                        pe.wait_ge(hT_ok, KD * (q - 1) + k + 1)
                    for t in range(4):
                        last = nc.tensor.transpose(ps[:, 6 + k, P * t:P * (t + 1)],
                                                   rows[:, q, t, P * k:P * (k + 1)], ident[:, :])
                    last.then_inc(rowsT_mm, 1)

            def modulation_bT():
                pe.wait_ge(ld_modB, 16)
                for m in range(3):
                    for n in range(KD):
                        at = (3 + m) * D + P * n
                        for k in range(KD):
                            nc.tensor.matmul(modTP[:, m, n, :], wmod_sb[:, k, at:at + P], c_silu[:, k, :, 0],
                                             start=(k == 0), stop=(k == KD - 1))

            def modulation_gate():
                for b in range(B):
                    for k in range(KD):
                        last = nc.tensor.matmul(ps[:, 4, D * b:D * (b + 1)], c_silu[:, k, b, :],
                                                wmod_sb[:, k, 2 * D:3 * D], start=(k == 0), stop=(k == KD - 1))
                last.then_inc(modB_mm, 1)

            def scores(i):
                n = HEADS * (i + 1)
                if i >= 4:
                    pe.wait_ge(diff_ok, (2, 4, 5, 6)[i - 4])
                if i == 4:
                    pe.wait_ge(hT_ok, KD * NB)
                for b in range(B):
                    q = B * (i // 4) + b
                    for k in range(KD):
                        last = nc.tensor.matmul(score_place(i)[:, b, :], hT[:, k, q, P * (i % 4):P * (i % 4 + 1)],
                                                W1[:, k, 0:n], start=(k == 0), stop=(k == KD - 1))
                last.then_inc(score_mm, 1)

            def turn_probs(i):
                pe.wait_ge(prob_ok, i + 1)
                if i >= 6:
                    pe.wait_ge(probT_ok, i - 1)
                for c, w in enumerate(widths(i)):
                    for b in range(B):
                        last = nc.tensor.transpose(probT_place(i, c)[:, P * b:P * (b + 1)],
                                                   step(i)[:, b, P * c:P * c + w], ident[:, :])
                last.then_inc(probT_mm, 1)

            def attend(i):
                pe.wait_ge(probT_ok, 4 if i in (2, 3) else i + 1)
                if i >= 6:
                    pe.wait_ge(x1_ok, i - len(BY_PE) - 1)
                ws = widths(i)
                for b in range(B):
                    for c, w in enumerate(ws):
                        last = nc.tensor.matmul(ps[:, att_bank(i), D * b:D * (b + 1)], probT[0:w, i % 4, c, b, :],
                                                W2[0:w, b, c, :], start=(c == 0), stop=(i not in BY_PE and c == len(ws) - 1))
                    if i in BY_PE:
                        last = nc.tensor.matmul(ps[:, att_bank(i), D * b:D * (b + 1)], ident[:, :], x[:, b, i, :],
                                                start=False, stop=True)
                last.then_inc(att_mm, 1)

            def turn_rows2(q):
                pe.wait_ge(rows2_ok, q + 1)
                if q == 0:
                    pe.wait_ge(rows2_half_ok, 1)
                if q == 2:
                    pe.wait_ge(x1_ok, W - len(BY_PE))
                for k in range(KD):
                    if q == 0:
                        pe.wait_ge(hT_ok, KD * (NB - 1) + k + 1)
                    elif q != 2:
                        pe.wait_ge(h2_full_ok, KD * (q - 1) + k + 1)
                    for t in range(4):
                        last = nc.tensor.transpose(ps[:, 6 + k, P * t:P * (t + 1)],
                                                   rows[:, q, t, P * k:P * (k + 1)], ident[:, :])
                    last.then_inc(rows2T_mm, 1)

            pe.wait_ge(ident_ok, 1)
            pe.wait_ge(pad_ok, 2)
            product(wq_sb, 0, ld_wq)
            turn_rows(0)
            modulation_bT()
            turn_rows(1)
            product_turned(0)
            pe.wait_ge(W1_ok, KD)
            pe.wait_ge(modA_ok, 1)
            pe.wait_ge(hT_ok, KD * B)
            for i in range(4):
                scores(i)
            modulation_gate()
            pe.wait_ge(pad_ok, 4)
            product(wo_sb, 1, ld_wo)
            turn_rows(2)
            product_turned(1)
            turn_rows(3)
            pe.wait_ge(W2T_ok, 1)
            for c in range(2):
                for k in range(KD):
                    last = nc.tensor.transpose(ps[:, 2, D * c + P * k:D * c + P * (k + 1)],
                                               W2T[:, k, P * c:P * (c + 1)], ident[:, :])
            last.then_inc(W2_mm, 1)
            pe.wait_ge(modB_ok, 2)
            for i in range(4):
                turn_probs(i)
            scores(4)
            scores(5)
            pe.wait_ge(W2_ok, B)
            for i in range(4):
                attend(i)
            scores(6)
            turn_rows2(0)
            scores(7)

            pe.wait_ge(diff_ok, W - 1)
            pe.wait_ge(x1_first_ok, len(BY_PE))

            def gate_up(q, s, nth, extra, up_split=0):
                u = q * (SETS * 4) + 4 * s
                for r in range(4):
                    if not nth and r == 1:
                        pe.wait_ge(diff_ok, W)
                    for hi, lo, bank, read, done in ((wg_hi, wg_lo, r % 2, silu_ok, gate_mm),
                                                     (wu_hi, wu_lo, 2 + r % 2, hid_ok, up_mm)):
                        if nth or r >= 2:
                            pe.wait_ge(read, u + r - 1)
                        if up_split and r == 0 and done is up_mm:
                            pe.wait_ge(w_first_ok, up_split)
                        for k in range(KD):
                            nc.tensor.matmul(ps[:, bank, :], lo[:, k, s, r, :], h2_hi[:, k, q, :],
                                             start=(k == 0), stop=False)
                            nc.tensor.matmul(ps[:, bank, :], hi[:, k, s, r, :], h2_hi[:, k, q, :],
                                             start=False, stop=False)
                        if not nth and r == 0 and done is gate_mm:
                            pe.wait_ge(h2_first_ok, KD)
                        for k in range(KD):
                            last = nc.tensor.matmul(ps[:, bank, :], hi[:, k, s, r, :], h2_lo[:, k, q, :],
                                                    start=False, stop=(k == KD - 1))
                        last.then_inc(done, 1)
                    if r in extra:
                        extra[r]()

            def down(unit, s, between=None):
                for r in range(4):
                    pe.wait_ge(kept_lo_ok, unit * 4 + r + 1)
                    for k in range(KD):
                        cols = slice(P * k, P * (k + 1))
                        nc.tensor.matmul(ps[:, 4 + k, :], wd_lo[:, s, r, cols], kept_hi[:, s, r, :],
                                         start=(s == 0 and r == 0), stop=False)
                        nc.tensor.matmul(ps[:, 4 + k, :], wd_hi[:, s, r, cols], kept_lo[:, s, r, :],
                                         start=False, stop=False)
                        last = nc.tensor.matmul(ps[:, 4 + k, :], wd_hi[:, s, r, cols], kept_hi[:, s, r, :],
                                                start=False, stop=(s == SETS - 1 and r == 3))
                    if r == 0 and between:
                        between()
                last.then_inc(down_mm, 1)

            def turn_y(yT_count):
                pe.wait_ge(yT_ok, yT_count)
                for t in range(4):
                    for k in range(KD):
                        last = nc.tensor.transpose(ps[:, 6 + t // 2, D * (t % 2) + P * k:D * (t % 2) + P * (k + 1)],
                                                   yT[:, k, P * t:P * (t + 1)], ident[:, :])
                    if t % 2:
                        last.then_inc(back_mm, 1)

            pe.wait_ge(h2_hi_ok, KD)
            pe.wait_ge(w_first_ok, 1)
            gate_up(0, 0, 0, {1: lambda: turn_probs(4), 2: lambda: (turn_rows2(1), turn_probs(5)),
                              3: lambda: turn_probs(6)}, up_split=2)
            pe.wait_ge(w_ok, 1)
            gate_up(0, 1, 1, {0: lambda: (pe.wait_ge(h2_full_ok, KD * 2), attend(4), turn_probs(7)),
                              1: lambda: attend(5), 2: lambda: attend(6), 3: lambda: attend(7)}, up_split=3)
            pe.wait_ge(probT_ok, W)
            pe.wait_ge(w_ok, 3)
            down(0, 0)
            pe.wait_ge(h2_ok, KD)
            gate_up(1, 0, 1, {})
            down(1, 1, between=lambda: turn_rows2(2))
            gate_up(1, 1, 1, {1: lambda: turn_rows2(3)})
            pe.wait_ge(yT_ok, KD)
            down(2, 0)
            pe.wait_ge(h2_full_ok, KD * NB)
            turn_y(KD)
            with pe.Fori(2, NB) as q:
                pe.wait_ge(h2_ok, q * KD)
                gate_up(q, 0, 1, {})
                down(q * SETS - 1, 1)
                gate_up(q, 1, 1, {})
                pe.wait_ge(yT_ok, q * KD)
                down(q * SETS, 0)
                turn_y(q * KD)
            down(NB * SETS - 1, 1)
            pe.wait_ge(y_ok, 2 * (NB - 1))
            pe.wait_ge(y_last_ok, 1)
            turn_y(NB * KD - 1)

        @block.vector
        def _(dve):
            steps = [0]

            def link(ins):
                steps[0] += 1
                ins.then_inc(dve_step, 1)
                dve.wait_ge(dve_step, steps[0])

            def rsqrt(dst, src, n, beside=()):
                def also(k):
                    if k < len(beside):
                        beside[k]()

                bits, half, yy = seed[:, 0:n], newton[:, 0, 0:n], newton[:, 1, 0:n]
                link(nc.vector.tensor_scalar(bits, src.bitcast(I32), 1, None, ALU.arith_shift_right))
                nc.vector.tensor_scalar(half, src, -0.5, None, ALU.mult)
                also(0)
                link(nc.vector.tensor_scalar(dst.bitcast(I32), bits, -1.0, float(RSQRT_SEED), ALU.mult, ALU.add))
                for turn in range(3):
                    also(3 * turn + 1)
                    link(nc.vector.tensor_tensor(yy, dst, dst, ALU.mult))
                    also(3 * turn + 2)
                    link(nc.vector.tensor_tensor(yy, yy, half, ALU.mult))
                    also(3 * turn + 3)
                    last = nc.vector.scalar_tensor_tensor(dst, yy, 1.5, dst, ALU.add, ALU.mult)
                    if turn < 2:
                        link(last)
                return last

            def tile_stats(q, t):
                return nc.vector.bn_stats(stats[:, 4 * q + t, :], x[:, q, t, :])

            def aggregate(tiles):
                for t in tiles:
                    last = nc.vector.bn_aggr(mv[:, t, :], stats[:, t, :])
                return last

            def variance(q0, nq, slot, tiles=None):
                a, b = 4 * q0, 4 * (q0 + nq)
                last = aggregate(tiles or range(a, b))
                link(last)
                n = slot(a)
                return nc.vector.tensor_scalar(var[:, n:n + b - a], mv[:, a:b, 1], EPS_LN, None, ALU.add)

            def mean_square(half):
                dve.wait_ge(sumsq_ok, 8 * (half + 1))
                n = rms_slot(8 * half)
                return nc.vector.tensor_scalar(var[:, n:n + 8], sumsq[:, 8 * half:8 * half + 8], 1.0 / D, EPS_RMS,
                                               ALU.mult, ALU.add)

            def norms(a, b, beside=()):
                rsqrt(rstd[:, a:b], var[:, a:b], b - a, beside).then_inc(norms_ok, 1)

            def centre_and_scale(q):
                for t in range(4):
                    n = 4 * q + t
                    last = nc.vector.scalar_tensor_tensor(rows[:, q, t, :], x[:, q, t, :], mv[:, n, 0:1],
                                                          mod[:, SCALE_A, q % B, :], ALU.subtract, ALU.mult)
                last.then_inc(scaled_ok, 1)

            def divide_and_shift(q):
                dve.wait_ge(scaled_ok, q + 1)
                for t in range(4):
                    n = rstd_slot(4 * q + t)
                    last = nc.vector.scalar_tensor_tensor(rows[:, q, t, :], rows[:, q, t, :], rstd[:, n:n + 1],
                                                          mod[:, SHIFT_A, q % B, :], ALU.mult, ALU.add)
                last.then_inc(rows_ok, 1)

            def normalise_half():
                dve.wait_ge(norms_ok, 4)
                dve.wait_ge(rowsT_mm, KD)
                dve.wait_ge(sumsq_ok, 4)
                for t in (2, 3):
                    n = rstd2_slot(t)
                    last = nc.vector.tensor_scalar(rows[:, 0, t, :], x[:, 0, t, :], mv[:, t, 0:1], rstd[:, n:n + 1],
                                                   ALU.subtract, ALU.mult)
                last.then_inc(rows2_half_ok, 1)

            dve.wait_ge(c_exp, 1)
            link(nc.vector.tensor_scalar(c_e[:, :, :], c_e[:, :, :], 1.0, None, ALU.add))
            link(nc.vector.reciprocal(c_e[:, :, :], c_e[:, :, :]))
            every = [P, KD, B, P]
            nc.vector.tensor_tensor(c_silu[:, :, :, :], c_sb[:, :, :].unsqueeze(3).broadcast_to(every),
                                    c_e[:, :, :].unsqueeze(3).broadcast_to(every), ALU.mult).then_inc(c_ok, 1)

            def row_stats(half):
                for q in range(B * half, B * (half + 1)):
                    dve.wait_ge(ld_x[q], 16)
                    for t in range(4):
                        last = tile_stats(q, t)
                link(last)
                return variance(B * half, B, rstd_slot)

            def scale_W1():
                def nothing():
                    pass

                def chunk(k):
                    dve.wait_ge(foldT_mm, 1)
                    nc.vector.tensor_scalar(W1[:, k, :].rearrange("p (j h) -> p j h", j=W),
                                            ps[:, 3, NK * k:NK * (k + 1)].rearrange("p (h j) -> p j h", j=W),
                                            wn[:, k:k + 1], SCALE, ALU.mult, ALU.mult).then_inc(W1_ok, 1)

                dve.wait_ge(ld_wn, 16)
                return nothing, nothing, nothing, lambda: chunk(0), lambda: chunk(1)

            def peaks(w):
                dve.wait_ge(ld_w[w], 16)
                nc.vector.tensor_reduce(peak[:, 2 + w:3 + w], raw[:, w, :], AX_X, ALU.max,
                                        apply_absolute_value=True).then_inc(peak_ok, 1)

            def bounds():
                s, a, m_gate, m_up, w_down_squares = (peaks_all[:, n:n + 1] for n in range(5))

                def step1():
                    dve.wait_ge(peaks_all_ok, 1)
                    nc.vector.scalar_tensor_tensor(bound[:, 0:1], a, 16.0, s, ALU.mult, ALU.add)
                    nc.vector.tensor_copy(bound[:, 1:3], peaks_all[:, 2:4])
                    nc.vector.tensor_scalar(root[:, :], w_down_squares.bitcast(I32), 1, None, ALU.arith_shift_right)
                    nc.vector.tensor_tensor(bound_t[:, 2:3], m_gate, m_up, ALU.mult)
                    nc.vector.tensor_tensor(bound_t[:, 0:1], a, s, ALU.add)

                def step2():
                    nc.vector.tensor_scalar(bound[:, 3:4].bitcast(I32), root[:, :], float(127 << 22), None, ALU.add)
                    nc.vector.scalar_tensor_tensor(bound_t[:, 1:2], bound_t[:, 0:1], 65536.0, bound_t[:, 0:1],
                                                   ALU.mult, ALU.mult)

                def step3():
                    nc.vector.tensor_tensor(bound[:, 4:5], bound_t[:, 1:2], bound_t[:, 2:3], ALU.mult)

                def step4():
                    nc.vector.tensor_scalar(expo[:, :], bound[:, :].bitcast(I32), 0x7F800000, None, ALU.bitwise_and)

                def step5():
                    nc.vector.tensor_scalar(expo[:, :], expo[:, :], float(64 << 23), None, ALU.max)

                def step6():
                    nc.vector.tensor_scalar(up2[:, :].bitcast(I32), expo[:, :], -1.0, float(268 << 23), ALU.mult, ALU.add)
                    nc.vector.tensor_scalar(down2[:, :].bitcast(I32), expo[:, :], float(14 << 23), None, ALU.subtract)

                def step7():
                    nc.vector.tensor_scalar(modT_up[:, :, :, :], modT[:, SHIFT_B:SCALE_B + 1, :, :], up2[:, 0:1], None, ALU.mult)
                    nc.vector.tensor_tensor(un_up[:, :], down2[:, 0:1], down2[:, 2:3], ALU.mult)
                    nc.vector.tensor_tensor(un_gate[:, :], down2[:, 0:1], down2[:, 1:2], ALU.mult)
                    nc.vector.tensor_tensor(un_y[:, :], down2[:, 3:4], down2[:, 4:5], ALU.mult)

                def step8():
                    nc.vector.tensor_tensor(un_up[:, :], un_up[:, :], up2[:, 4:5], ALU.mult).then_inc(scale_ok, 1)

                return step1, step2, step3, step4, step5, step6, step7, step8

            def split_weight(n):
                dve.wait_ge(w_hi_ok, n + 1)
                w = PIECES[n][0]
                nc.vector.scalar_tensor_tensor(piece(part_lo, n), piece(raw, n), up2[:, 1 + w:2 + w],
                                               piece(part_hi, n), ALU.mult, ALU.subtract).then_inc(w_first_ok, 1)

            def subtract_top(*steps):
                for i in steps:
                    dve.wait_ge(score_mm, i + 1 if i >= 4 else 2 * (i // 2) + 2)
                    last = nc.vector.tensor_reduce(top[:, i % 4, :, :], cut(score_place(i)).rearrange("p b j h -> p b h j"),
                                                   AX_X, ALU.max)
                link(last)
                for i in steps:
                    nc.vector.tensor_tensor(cut(step(i)), cut(score_place(i)), over(top[:, i % 4, :, :], i),
                                            ALU.subtract).then_inc(diff_ok, 1)

            def divide(*steps):
                for i in steps:
                    dve.wait_ge(exp_ok, B * (i + 1))
                    last = nc.vector.tensor_reduce(total[:, i % 4, :, :], cut(step(i)).rearrange("p b j h -> p b h j"),
                                                   AX_X, ALU.add)
                link(last)
                first = steps[0] % 4
                last = nc.vector.reciprocal(inv[:, first:first + len(steps), :, :], total[:, first:first + len(steps), :, :])
                if steps[0] in BY_POOL:
                    last.then_inc(inv_ok, 1)
                    return
                link(last)
                for i in steps:
                    nc.vector.tensor_tensor(cut(step(i)), cut(step(i)), over(inv[:, i % 4, :, :], i),
                                            ALU.mult).then_inc(prob_ok, 1)

            def add_attention(i):
                f, t = i // 4, i % 4
                if i in BY_PE:
                    dve.wait_ge(x1_first_ok, i + 1)
                else:
                    dve.wait_ge(att_mm, i + 1)
                    old = x[:, B * f:B * (f + 1), t, :]
                    nc.vector.tensor_tensor(old, ps[:, att_bank(i), :].rearrange("p (b d) -> p b d", b=B), old,
                                            ALU.add).then_inc(x1_ok, 1)
                    dve.wait_ge(x1_ok, i - len(BY_PE) + 1)
                if t == 3:
                    aggregate([4 * (B * f + b) + before for b in range(B) for before in range(t)])
                for b in range(B):
                    last = tile_stats(B * f + b, t)
                if t < 3:
                    last.then_inc(stats_ok, 1)
                    dve.wait_ge(stats_ok, 3 * f + t + 1)
                else:
                    link(last)
                    link(variance(B * f, B, rstd2_slot, [4 * (B * f + b) + t for b in range(B)]))
                    n = rstd2_slot(8 * f)
                    link(rsqrt(rstd[:, n:n + 8], var[:, n:n + 8], 8))
                    nc.vector.scalar_tensor_tensor(shifted[:, 8 * f:8 * f + 8], mv[:, 8 * f:8 * f + 8, 0], -1.0,
                                                   rstd[:, n:n + 8], ALU.mult, ALU.mult).then_inc(norms_ok, 1)

            def split_h2_first():
                for k in range(KD):
                    dve.wait_ge(h2_full_ok, k + 1)
                    nc.vector.tensor_tensor(h2_lo[:, k, 0, :], h2_full(0)[:, k, :], h2_hi[:, k, 0, :],
                                            ALU.subtract).then_inc(h2_first_ok, 1)

            link(row_stats(0))
            norms(0, 8)
            dve.wait_ge(norms_ok, 1)
            dve.wait_ge(modA_ok, 1)
            centre_and_scale(0)
            divide_and_shift(0)
            centre_and_scale(1)
            divide_and_shift(1)
            row_stats(1)
            link(mean_square(0))
            norms(8, 24, scale_W1())
            subtract_top(0, 1)
            centre_and_scale(2)
            subtract_top(2, 3)
            dve.wait_ge(norms_ok, 2)
            divide_and_shift(2)
            divide(0, 1)
            divide(2, 3)
            centre_and_scale(3)
            divide_and_shift(3)
            dve.wait_ge(modB_ok, 2)
            for m in (SHIFT_B, SCALE_B):
                nc.vector.tensor_reduce(peak[:, m:m + 1], modT[:, m, :, :], AX_XY, ALU.max,
                                        apply_absolute_value=True).then_inc(peak_ok, 1)
            peaks(0)
            peaks(1)
            subtract_top(4)
            link(mean_square(1))
            norms(24, 32, bounds())
            add_attention(0)
            subtract_top(5)
            for i in range(1, 4):
                add_attention(i)
            normalise_half()
            subtract_top(6)
            dve.wait_ge(scale_ok, 1)
            split_weight(0)
            split_weight(1)
            split_h2_first()
            subtract_top(7)
            divide(4)

            def hiddens(q, s, nth, extra):
                unit = q * SETS + s
                a = mag[:, s, :, :]

                def beat(first, r, members):
                    n = members.stop - members.start
                    nc.vector.tensor_tensor(beats[:, first:first + n, :], a[:, members, :],
                                            a[:, r:r + 1, :].broadcast_to([P, n, T]), ALU.is_ge).then_inc(beats_ok, 1)

                def combine(out, x0, x1, op, done):
                    nc.vector.tensor_tensor(out, x0, x1, op).then_inc(done, 1)

                def keep(r, op, limit):
                    dve.wait_ge(wins_ok, unit * 4 + r + 1)
                    nc.vector.scalar_tensor_tensor(kept[:, s, r, :], wins[:, r, :], limit, hid[:, s, r, :],
                                                   op, ALU.mult).then_inc(kept_ok, 1)

                for r in range(4):
                    dve.wait_ge(silu_ok, unit * 4 + r + 1)
                    dve.wait_ge(up_mm, unit * 4 + r + 1)
                    nc.vector.scalar_tensor_tensor(hid[:, s, r, :], sg[:, r % 2, :], un_up[:, 0:1], ps[:, 2 + r % 2, :],
                                                   ALU.mult, ALU.mult).then_inc(hid_ok, 1)
                    if r in extra:
                        extra[r]()
                    if r in (1, 2):
                        dve.wait_ge(mag_ok, unit * 4 + r + 1)
                        beat(r - 1, r, slice(0, r))
                dve.wait_ge(beats_ok, unit * 5 + 2)
                combine(pairs[:, 0, :], beats[:, 0, :], beats[:, 1, :], ALU.add, pairs_ok)
                combine(pairs[:, 1, :], beats[:, 2, :], beats[:, 0, :], ALU.subtract, pairs_ok)
                combine(pairs[:, 2, :], beats[:, 1, :], beats[:, 2, :], ALU.add, pairs_ok)
                dve.wait_ge(mag_ok, unit * 4 + 4)
                dve.wait_ge(pairs_ok, unit * 4 + 3)
                if nth:
                    dve.wait_ge(kept_lo_ok, 4 * unit - 4)
                beat(3, 3, slice(0, 1))
                dve.wait_ge(beats_ok, unit * 5 + 3)
                combine(wins[:, 0, :], pairs[:, 0, :], beats[:, 3, :], ALU.add, wins_ok)
                keep(0, ALU.is_ge, 2.0)
                beat(4, 3, slice(1, 2))
                dve.wait_ge(beats_ok, unit * 5 + 4)
                combine(wins[:, 1, :], pairs[:, 1, :], beats[:, 4, :], ALU.add, wins_ok)
                keep(1, ALU.is_ge, 1.0)
                beat(5, 3, slice(2, 3))
                combine(pairs[:, 3, :], beats[:, 3, :], beats[:, 4, :], ALU.add, pairs_ok)
                dve.wait_ge(beats_ok, unit * 5 + 5)
                combine(wins[:, 2, :], beats[:, 5, :], pairs[:, 2, :], ALU.subtract, wins_ok)
                dve.wait_ge(pairs_ok, unit * 4 + 4)
                combine(wins[:, 3, :], pairs[:, 3, :], beats[:, 5, :], ALU.add, wins_ok)
                keep(2, ALU.is_ge, 0.0)
                keep(3, ALU.is_le, 1.0)

            def add_ffn(q):
                for m in range(2):
                    dve.wait_ge(back_mm, q * 2 + m + 1)
                    old = x[:, q, 2 * m:2 * m + 2, :]
                    nc.vector.tensor_tensor(old, ps[:, 6 + m, :].rearrange("p (t d) -> p t d", t=2), old,
                                            ALU.add).then_inc(y_ok, 1)

            hiddens(0, 0, 0, {0: lambda: divide(5), 1: lambda: divide(6), 2: lambda: (divide(7), split_weight(3))})
            hiddens(0, 1, 0, {1: lambda: add_attention(4), 2: lambda: add_attention(5), 3: lambda: add_attention(6)})
            hiddens(1, 0, 1, {0: lambda: add_attention(7)})
            hiddens(1, 1, 1, {})
            add_ffn(0)
            with dve.Fori(2, NB) as q:
                hiddens(q, 0, 1, {})
                hiddens(q, 1, 1, {})
                add_ffn(q - 1)
            dve.wait_ge(down_mm, SETS * NB)
            nc.vector.tensor_scalar(yT[:, 1, :], ps[:, 5, :], y_scale[:, 1, NB - 1:NB], None, ALU.mult).then_inc(y_last_ok, 1)
            add_ffn(NB - 1)


def kernel(L0_attn_seq, L0_attn_w_norm, L0_attn_w_qkv, L0_attn_w_out, L0_attn_pm, L0_ffn_w_gate, L0_ffn_w_up,
           L0_ffn_w_down, L0_c, L0_wmod):
    import numpy as _np
    import concourse.bacc as _bacc
    from concourse import mybir as _mybir
    from concourse.bass_utils import run_bass_kernel_spmd as _run

    D = L0_attn_seq.shape[2]
    windows = L0_attn_seq.shape[1] // SEGMENT
    heads_in = HEADS * DH

    def memory(m):
        rows = _np.asarray(L0_attn_pm)[m].reshape(HEADS // 2, 2, MEM, DH)[:, :, :windows]
        return rows.transpose(1, 3, 0, 2).reshape(2 * DH, HEADS // 2, windows)

    def grouped(w):
        w = _np.asarray(w)
        return w.reshape(w.shape[0], 2, P, 4).transpose(0, 1, 3, 2)

    laid = {
        "seq": L0_attn_seq,
        "w_norm": L0_attn_w_norm,
        "wqT": _np.asarray(L0_attn_w_qkv)[:, :heads_in].T,
        "w_out": L0_attn_w_out,
        "pmkT": memory(0),
        "pmvT": memory(1),
        "w_gate": grouped(L0_ffn_w_gate),
        "w_up": grouped(L0_ffn_w_up),
        "w_down": L0_ffn_w_down,
        "cT": _np.asarray(L0_c).T,
        "w_mod": L0_wmod,
    }
    nc = _bacc.Bacc("TRN2", target_bir_lowering=False, num_devices=1)
    arrays, args = {}, []
    for name, a in laid.items():
        a = _np.ascontiguousarray(a)
        arrays[f"in_{name}"] = a
        args.append(nc.dram_tensor(f"in_{name}", a.shape, _mybir.dt.from_np(a.dtype), kind="ExternalInput").ap())
    args.append(nc.dram_tensor("out_0", L0_attn_seq.shape, _mybir.dt.float32, kind="ExternalOutput").ap())
    adaln_block(nc, *args)
    return _run(nc, [arrays], core_ids=[0]).results[0]["out_0"]
```
